# Optimizing a Trainium2 kernel written in Bass

```python
import numpy as np
import jax
import jax.numpy as jnp

def _softmax(x, axis=-1):
    return jax.nn.softmax(x, axis=axis)

def _gelu(x):
    return jax.nn.gelu(x, approximate=True)

def _silu(x):
    return jax.nn.silu(x)

def _sigmoid(x):
    return jax.nn.sigmoid(x)

def _layernorm(x, axis=-1, eps=1e-05):
    m = jnp.mean(x, axis=axis, keepdims=True)
    v = jnp.var(x, axis=axis, keepdims=True)
    return (x - m) / jnp.sqrt(v + eps)

def _scatter_add(tgt, idx, src, axis=0):
    return tgt.at[idx].add(src)

def _segment_sum(src, seg, n):
    return jax.ops.segment_sum(src, seg, n)
kernel_name = 'mk_prb_d1_jaxref_r8_6b6292'

def setup_inputs(seed: int=0):
    np.random.seed(seed)
    _w = jnp.asarray

    def _L0_attn_setup():
        import jax, jax.numpy as jnp
        import numpy as np
        import math
        N_HEAD = 16
        N_EMBD = 256
        HEAD_DIM = 128
        N_LAYER = 24
        EPS = 1e-05

        def _get_alibi_slopes(n_heads):

            def pow2(n):
                start = 2 ** (-2 ** (-(math.log2(n) - 3)))
                return [start * start ** i for i in range(n)]
            if math.log2(n_heads).is_integer():
                return pow2(n_heads)
            c = 2 ** math.floor(math.log2(n_heads))
            s = pow2(c)
            extra = _get_alibi_slopes(2 * c)
            return s + extra[0::2][:n_heads - c]
        ALIBI_SLOPES = jnp.asarray(np.array(_get_alibi_slopes(N_HEAD), dtype=np.float32))

        def rmsnorm(x, w, eps=EPS):
            xf = x.astype(jnp.float32)
            out = xf * jax.lax.rsqrt(jnp.mean(xf * xf, axis=-1, keepdims=True) + eps)
            return (out * w.astype(jnp.float32)).astype(x.dtype)
        key = jax.random.key(seed)
        ks = jax.random.split(key, 8)
        B, T, C, H, D = (2, 256, N_EMBD, N_HEAD, HEAD_DIM)
        sc = 1.0 / math.sqrt(C)
        proj_std = 0.5 / math.sqrt(C) / math.sqrt(N_LAYER)
        return {'x': jax.random.normal(ks[0], (B, T, C), jnp.float32), 'Wq': jax.random.normal(ks[1], (C, H * D), jnp.float32) * sc, 'Wk': jax.random.normal(ks[2], (C, H * D), jnp.float32) * sc, 'Wv': jax.random.normal(ks[3], (C, H * D), jnp.float32) * sc, 'Wproj': jax.random.normal(ks[4], (H * D, C), jnp.float32) * proj_std, 'q_rms_w': jnp.ones((D,), jnp.float32), 'k_rms_w': jnp.ones((D,), jnp.float32), 'subln_w': jnp.ones((D,), jnp.float32)}
    _L0_attn_in = _L0_attn_setup()

    def _L0_ffn_setup():
        import jax, jax.numpy as jnp
        import numpy as np
        _FP8_DTYPE = jnp.float8_e4m3fn
        _FP8_MAX = 448.0
        key = jax.random.key(seed)
        k_x, k_w = jax.random.split(key)
        B, S, IN, OUT = (2, 1024, 256, 256)
        x = jax.random.normal(k_x, (B, S, IN), dtype=jnp.float32)
        w_f32 = jax.random.normal(k_w, (OUT, IN), dtype=jnp.float32) * 0.02
        weight = w_f32.astype(_FP8_DTYPE)
        weight_scale = jnp.asarray(1.5, dtype=jnp.float32)
        input_scale = jnp.asarray(0.75, dtype=jnp.bfloat16)
        return {'x': x, 'weight': weight, 'weight_scale': weight_scale, 'input_scale': input_scale}
    _L0_ffn_in = _L0_ffn_setup()
    _d = {'L0_attn_x': _L0_attn_in['x'], 'L0_attn_Wq': _L0_attn_in['Wq'], 'L0_attn_Wk': _L0_attn_in['Wk'], 'L0_attn_Wv': _L0_attn_in['Wv'], 'L0_attn_Wproj': _L0_attn_in['Wproj'], 'L0_attn_q_rms_w': _L0_attn_in['q_rms_w'], 'L0_attn_k_rms_w': _L0_attn_in['k_rms_w'], 'L0_attn_subln_w': _L0_attn_in['subln_w'], 'L0_ffn_weight': _L0_ffn_in['weight'], 'L0_ffn_weight_scale': _L0_ffn_in['weight_scale'], 'L0_ffn_input_scale': _L0_ffn_in['input_scale']}
    _x0 = _d['L0_attn_x']
    _d['L0_attn_x'] = jax.random.normal(jax.random.fold_in(jax.random.key(seed), 1), (1, 1024, 256), dtype=_x0.dtype)
    del _x0
    return _d

def reference(L0_attn_x, L0_attn_Wq, L0_attn_Wk, L0_attn_Wv, L0_attn_Wproj, L0_attn_q_rms_w, L0_attn_k_rms_w, L0_attn_subln_w, L0_ffn_weight, L0_ffn_weight_scale, L0_ffn_input_scale):

    def _L0_attn_ref(x, Wq, Wk, Wv, Wproj, q_rms_w, k_rms_w, subln_w):
        import jax, jax.numpy as jnp
        import numpy as np
        import math
        N_HEAD = 16
        N_EMBD = 256
        HEAD_DIM = 128
        N_LAYER = 24
        EPS = 1e-05

        def _get_alibi_slopes(n_heads):

            def pow2(n):
                start = 2 ** (-2 ** (-(math.log2(n) - 3)))
                return [start * start ** i for i in range(n)]
            if math.log2(n_heads).is_integer():
                return pow2(n_heads)
            c = 2 ** math.floor(math.log2(n_heads))
            s = pow2(c)
            extra = _get_alibi_slopes(2 * c)
            return s + extra[0::2][:n_heads - c]
        ALIBI_SLOPES = jnp.asarray(np.array(_get_alibi_slopes(N_HEAD), dtype=np.float32))

        def rmsnorm(x, w, eps=EPS):
            xf = x.astype(jnp.float32)
            out = xf * jax.lax.rsqrt(jnp.mean(xf * xf, axis=-1, keepdims=True) + eps)
            return (out * w.astype(jnp.float32)).astype(x.dtype)
        B, T, C = x.shape
        H, D = (N_HEAD, HEAD_DIM)
        q = (x @ Wq).reshape(B, T, H, D)
        k = (x @ Wk).reshape(B, T, H, D)
        v = (x @ Wv).reshape(B, T, H, D)
        q = rmsnorm(q, q_rms_w)
        k = rmsnorm(k, k_rms_w)
        idx = jnp.arange(T)
        dist = jnp.maximum(idx[:, None] - idx[None, :], 0).astype(jnp.float32)
        bias = -dist[None, :, :] * ALIBI_SLOPES[:, None, None]
        causal = idx[:, None] >= idx[None, :]
        scale = 1.0 / math.sqrt(D)
        scores = jnp.einsum('bthd,bshd->bhts', q, k) * scale + bias[None]
        scores = jnp.where(causal[None, None], scores, -jnp.inf)
        attn = jax.nn.softmax(scores, axis=-1)
        y = jnp.einsum('bhts,bshd->bhtd', attn, v)
        y = rmsnorm(y, subln_w)
        y = y.transpose(0, 2, 1, 3).reshape(B, T, H * D)
        return y @ Wproj

    def _L0_ffn_ref(x, weight, weight_scale, input_scale):
        import jax, jax.numpy as jnp
        import numpy as np
        _FP8_DTYPE = jnp.float8_e4m3fn
        _FP8_MAX = 448.0
        orig_dtype = x.dtype
        w = weight.astype(orig_dtype) * weight_scale.astype(orig_dtype)
        s_f32 = input_scale.astype(jnp.float32)
        x_scaled = x.astype(jnp.float32) / s_f32
        x_fp8 = jnp.clip(x_scaled, -_FP8_MAX, _FP8_MAX).astype(_FP8_DTYPE)
        x_qdq = x_fp8.astype(orig_dtype) * s_f32.astype(orig_dtype)
        return jnp.einsum('bsi,oi->bso', x_qdq, w)
    x = L0_attn_x
    xn = _layernorm(x, axis=-1)
    x = x + _L0_attn_ref(xn, L0_attn_Wq, L0_attn_Wk, L0_attn_Wv, L0_attn_Wproj, L0_attn_q_rms_w, L0_attn_k_rms_w, L0_attn_subln_w) + _L0_ffn_ref(xn, L0_ffn_weight, L0_ffn_weight_scale, L0_ffn_input_scale)
    return x

_drawn_inputs = setup_inputs


def setup_inputs(seed=0):
    import zlib

    import numpy as np

    out = dict(_drawn_inputs(seed))
    spreads = {'L0_attn_q_rms_w': (1.0, 0.2),
     'L0_attn_k_rms_w': (1.0, 0.2),
     'L0_attn_subln_w': (1.0, 0.2)}
    factors = {}
    for name, (base, spread) in spreads.items():
        noise = np.random.default_rng([zlib.crc32(name.encode()), seed]).standard_normal(out[name].shape)
        drawn = base * np.exp(spread * noise) if base else spread * noise
        out[name] = jnp.asarray(drawn.astype(out[name].dtype))
    for name, factor in factors.items():
        out[name] = (out[name] * factor).astype(out[name].dtype)
    return out
```

```python
import numpy as np
import concourse.bass as bass
from concourse import mybir
from contextlib import ExitStack



def build_block(nc, x, wq, wk, wv, wproj, q_w, k_w, sub_w, ffn_w, ffn_ws, ffn_xs, out):
    f32, f32r, bf16 = mybir.dt.float32, mybir.dt.float32r, mybir.dt.bfloat16
    i32, u8 = mybir.dt.int32, mybir.dt.uint8
    ALU, ACT, AX = mybir.AluOpType, mybir.ActivationFunctionType, mybir.AxisListType

    P = 128
    T, C = x.shape[0], x.shape[1]
    D = q_w.shape[0]
    H = wq.shape[1] // D
    NT = T // P
    KT = C // P
    NPAIR = NT // 2
    EPS = 1e-5
    SCALE = float(D) ** -0.5
    BIG = 1e30
    E4M3_MAX = 448.0

    ORDER = [7, 0, 6, 1, 5, 2, 4, 3]
    GROUPS = [sorted(ORDER[:4], reverse=True), sorted(ORDER[4:], reverse=True)]
    RANK = {i: (g, GROUPS[g].index(i)) for g in range(2) for i in GROUPS[g]}
    CHUNKS = [[(j, min(j + 4, i + 1)) for j in range(0, i + 1, 4)] for i in ORDER]
    CHUNK0 = [sum(len(c) for c in CHUNKS[:s]) for s in range(NT + 1)]
    CPH = CHUNK0[NT]

    MISC = ["qkT0", "ss1", "qkT1", "qkT2", "proj1a", "qkT3", "proj1b", "ss0", "proj0a", "proj0b"]
    MISC_FIRST = [m for m in MISC if m not in ("ss1", "proj1a", "proj1b")]
    MISC_LAST = [m for m in MISC if not m.startswith("qkT")]
    MISC_TAIL = ["ss1", "proj1a", "proj1b"]

    def misc_done(h, job):
        if isinstance(h, int) and h < 0:
            return int(job[3]) + 1
        if isinstance(h, int) and h == 0:
            return NPAIR + MISC_FIRST.index(job) + 1
        base = NPAIR + len(MISC_FIRST) + (h - 1) * len(MISC)
        if isinstance(h, int) and h == H - 1:
            return base + MISC_LAST.index(job) + 1
        if isinstance(h, int) and h == H:
            return base - len(MISC) + len(MISC_LAST) + MISC_TAIL.index(job) + 1
        return base + MISC.index(job) + 1

    def past(eng, sem, count):
        if not isinstance(count, int) or count > 0:
            eng.wait_ge(sem, count)

    ctx = ExitStack()
    with ctx:
        def sb(name, shape, dt=f32):
            return ctx.enter_context(nc.sbuf_tensor(name, shape, dt))

        def pb(name, shape, dt=f32):
            return ctx.enter_context(nc.psum_tensor(name, shape, dt))

        def sem(name):
            return ctx.enter_context(nc.semaphore(name))

        ident = sb("ident", [P, P])
        ident_b = sb("ident_b", [P, P], bf16)
        ones = sb("ones", [P, 1])
        minus_half = sb("minus_half", [P, NT])
        slopes = sb("slopes", [P, H])
        dist = sb("dist", [P, T])
        acc = sb("acc", [P, NT, C])
        xT_hi = sb("xT_hi", [P, KT, T], f32r)
        xT_lo = sb("xT_lo", [P, KT, T], f32r)
        w_raw = sb("w_raw", [P, 2, KT, 3 * D])
        w_hi = sb("w_hi", [P, 2, KT, 3 * D], f32r)
        w_lo = sb("w_lo", [P, 2, KT, 3 * D], f32r)
        wp_raw = sb("wp_raw", [P, 2, C])
        wp_hi = sb("wp_hi", [P, 2, C], f32r)
        wp_lo = sb("wp_lo", [P, 2, C], f32r)
        stage = sb("stage", [P, 2, 2, 3 * D])
        squares = sb("squares", [P, 2, 2 * D])
        qk_ms = sb("qk_ms", [P, 2, 4])
        qk_r = sb("qk_r", [P, 2, 4])
        qk_n = sb("qk_n", [P, 2, 2, 2, D])
        qT_hi = sb("qT_hi", [P, 2, T], f32r)
        qT_lo = sb("qT_lo", [P, 2, T], f32r)
        kT_hi = sb("kT_hi", [P, 2, T], f32r)
        kT_lo = sb("kT_lo", [P, 2, T], f32r)
        v_hi = sb("v_hi", [P, 2, NT, D], f32r)
        v_lo = sb("v_lo", [P, 2, NT, D], f32r)
        bias = sb("bias", [P, 2, T])
        probs = sb("probs", [P, 2, T])
        neg_max = sb("neg_max", [P, 2, NT])
        row_sum = sb("row_sum", [P, 2, 2, 4])
        pT_hi = [sb(f"pT_hi{g}", [P, GROUPS[g][0] + 1, 4 * P], f32r) for g in range(2)]
        pT_lo = [sb(f"pT_lo{g}", [P, GROUPS[g][0] + 1, 4 * P], f32r) for g in range(2)]
        yT_hi = sb("yT_hi", [P, 2, 4 * P], f32r)
        yT_lo = sb("yT_lo", [P, 2, 4 * P], f32r)
        y_sq = sb("y_sq", [P, 2, 4 * P])
        y_ms = sb("y_ms", [P, 2, 4])
        y_el2 = sb("y_el2", [P, 2, 4])
        y_r = sb("y_r", [P, 2, 4])
        q_col = sb("q_col", [P, 4])
        stats = sb("stats", [P, NT, 6])
        mean_var = sb("mean_var", [P, NT, 2])
        rstd = sb("rstd", [P, NT])
        xs_b = sb("xs_b", [P, 1], bf16)
        ffn_s = sb("ffn_s", [P, 4])
        w8 = sb("w8", [P, KT, C], mybir.dt.from_np(np.dtype("uint8")))
        wb = sb("wb", [P, KT, C], bf16)
        w8T = sb("w8T", [P, KT, C], bf16)
        xqT = sb("xqT", [P, KT, T], bf16)

        score_big = pb("score_big", [P, 1024])
        score_small = pb("score_small", [P, 512])
        pT_ps = [pb(f"pT_ps{b}", [P, 512]) for b in range(2)]
        yT_ps = pb("yT_ps", [P, 512])
        qkv_ps = pb("qkv_ps", [P, 512])
        misc = pb("misc", [P, 512])

        x_loaded = sem("x_loaded")
        small_loaded = sem("small_loaded")
        w8_loaded = sem("w8_loaded")
        w_loaded = [sem(f"w_loaded{b}") for b in range(2)]
        wp_loaded = [sem(f"wp_loaded{b}") for b in range(2)]
        w_split = sem("w_split")
        wp_split = sem("wp_split")
        const_ready = sem("const_ready")
        pool_step = sem("pool_step")
        dve_step = sem("dve_step")
        xn_ready = sem("xn_ready")
        xT_ready = sem("xT_ready")
        xT_hi_done = sem("xT_hi_done")
        xT_read = sem("xT_read")
        var_ready = sem("var_ready")
        rstd_ready = sem("rstd_ready")
        wb_ready = sem("wb_ready")
        w8T_ready = sem("w8T_ready")
        w8T_read = sem("w8T_read")
        xq_ready = sem("xq_ready")
        ffn_ready = sem("ffn_ready")
        ffn_added = sem("ffn_added")
        qkv_ready = sem("qkv_ready")
        qkv_read = sem("qkv_read")
        qk_squared = sem("qk_squared")
        qk_meansq = sem("qk_meansq")
        qk_normed = sem("qk_normed")
        qk_summed = sem("qk_summed")
        pool_r = sem("pool_r")
        pool_w_hi = sem("pool_w_hi")
        pool_wp_scaled = sem("pool_wp_scaled")
        pool_wp_hi = sem("pool_wp_hi")
        wq_col_ready = sem("wq_col_ready")
        qkT_ready = sem("qkT_ready")
        qkT_hi_done = sem("qkT_hi_done")
        v_hi_done = sem("v_hi_done")
        v_split = sem("v_split")
        bias_ready = sem("bias_ready")
        scores_ready = sem("scores_ready")
        scores_masked = sem("scores_masked")
        probs_ready = sem("probs_ready")
        pT_ready = sem("pT_ready")
        pT_hi_done = sem("pT_hi_done")
        pT_split = sem("pT_split")
        yT_ready = sem("yT_ready")
        y_hi_done = sem("y_hi_done")
        y_squared = sem("y_squared")
        y_split = sem("y_split")
        ss_ready = sem("ss_ready")
        el2_ready = sem("el2_ready")
        y_normed = sem("y_normed")
        proj_ready = sem("proj_ready")
        misc_read = sem("misc_read")
        stored = sem("stored")

        block = ctx.enter_context(nc.Block())

        wq_v = wq.rearrange("(k p) (h d) -> p k h d", p=P, d=D)
        wk_v = wk.rearrange("(k p) (h d) -> p k h d", p=P, d=D)
        wv_v = wv.rearrange("(k p) (h d) -> p k h d", p=P, d=D)
        wp_v = wproj.rearrange("(h p) c -> p h c", p=P)
        x_v = x.rearrange("(t p) c -> p t c", p=P)
        out_v = out.rearrange("(t p) c -> p t c", p=P)

        def over_heads(eng, body):
            body(0, 0)
            body(1, 1)
            with eng.Fori(1, H // 2 - 1) as pair:
                body(pair * 2, 0)
                body(pair * 2 + 1, 1)
            body(H - 2, 0)
            body(H - 1, 1)

        def bias_xn(t):
            return bias[:, t // 4, (t % 4) * C:(t % 4 + 1) * C]

        def is_last(h):
            return isinstance(h, int) and h == H - 1

        def score_at(i):
            w = (i + 1) * P
            if i < 4:
                return score_small, 0, [(0, w)]
            if w == 640:
                return score_big, 128, [(0, 384), (384, 640)]
            return score_big, 0, [(0, 512), (512, w)]

        @block.sync
        def _(sp):
            for t in range(0, NT, 2):
                sp.dma_start(acc[:, t:t + 2, :], x_v[:, t:t + 2, :]).then_inc(x_loaded, 16)

            def load_w(h, par):
                for n, w in enumerate((wq_v, wk_v, wv_v)):
                    sp.dma_start(w_raw[:, par, :, n * D:(n + 1) * D], w[:, :, h, :]).then_inc(w_loaded[par], 16)

            def load_wp(h, par):
                sp.dma_start(wp_raw[:, par, :], wp_v[:, h, :]).then_inc(wp_loaded[par], 16)

            load_w(0, 0)
            sp.dma_start(q_col[:, 0:1], q_w).then_inc(small_loaded, 16)
            sp.dma_start(q_col[:, 1:2], k_w).then_inc(small_loaded, 16)
            sp.dma_start(q_col[:, 3:4], sub_w).then_inc(small_loaded, 16)
            sp.dma_start(xs_b[:, :], ffn_xs.broadcast_to([P, 1])).then_inc(small_loaded, 16)
            sp.dma_start(ffn_s[:, 2:3], ffn_ws.broadcast_to([P, 1])).then_inc(small_loaded, 16)
            sp.dma_start(w8[:, :, :], ffn_w.rearrange("(k p) i -> p k i", p=P)).then_inc(w8_loaded, 16)
            load_w(1, 1)
            load_wp(0, 0)

            def head(h, par):
                if not (isinstance(h, int) and h + 2 >= H):
                    sp.wait_ge(w_split, h + 1)
                    load_w(h + 2, par)
                if not is_last(h):
                    past(sp, wp_split, h)
                    load_wp(h + 1, 1 - par)

            over_heads(sp, head)
            for g in range(2):
                sp.wait_ge(misc_read, misc_done(H - 1, "proj0b") if g == 0 else misc_done(H, "proj1b"))
                for i in GROUPS[g]:
                    sp.dma_start(out_v[:, i, :], acc[:, i, :]).then_inc(stored, 16)
            sp.wait_ge(stored, 16 * NT)

        @block.gpsimd
        def _(pool):
            steps = [0]

            def link(ins):
                steps[0] += 1
                ins.then_inc(pool_step, 1)
                pool.wait_ge(pool_step, steps[0])

            link(pool.memset(ident[:, :], 0.0))
            pool.affine_select(out=ident[:, :], in_=ident[:, :], compare_op=ALU.not_equal, fill=1.0, base=0,
                               pattern=[[-1, P]], channel_multiplier=1).then_inc(const_ready, 1)
            pool.memset(minus_half[:, :], -0.5)
            pool.wait_ge(const_ready, 1)
            pool.tensor_copy(ident_b[:, :], ident[:, :]).then_inc(const_ready, 1)
            pool.memset(ones[:, :], 1.0)
            for h in range(H):
                pool.memset(slopes[:, h:h + 1], float(np.float32(2.0 ** (-0.5 * (h + 1)))))
            link(pool.iota(dist[:, :], pattern=[[-1, T]], base=T - P, channel_multiplier=1,
                           allow_small_or_imprecise_dtypes=True))
            pool.affine_select(out=dist[:, :], in_=dist[:, :], compare_op=ALU.is_ge, fill=BIG, base=T - P,
                               pattern=[[-1, T]], channel_multiplier=1).then_inc(const_ready, 1)

            pool.wait_ge(var_ready, 1)
            pool.tensor_tensor(rstd[:, :], rstd[:, :], minus_half[:, :], ALU.pow).then_inc(rstd_ready, 1)

            def split_w(h, par):
                pool.wait_ge(w_loaded[par], 48 * (h // 2 + 1) if isinstance(h, int) else (h - par) * 24 + 48)
                past(pool, qkv_ready, (h - 1) * NT)
                pool.nop(nofuse=True)
                pool.tensor_copy(w_hi[:, par], w_raw[:, par]).then_inc(pool_w_hi, 1)
                pool.wait_ge(pool_w_hi, h + 1)
                pool.tensor_tensor(w_lo[:, par], w_raw[:, par], w_hi[:, par].bitcast(f32),
                                   ALU.subtract).then_inc(w_split, 1)

            def split_wp(h, par):
                pool.wait_ge(wp_loaded[par], 16 * (h // 2 + 1) if isinstance(h, int) else (h - par) * 8 + 16)
                past(pool, proj_ready, (h - 1) * 4)
                pool.nop(nofuse=True)
                pool.tensor_scalar(wp_raw[:, par], wp_raw[:, par], q_col[:, 3:4], None,
                                   ALU.mult).then_inc(pool_wp_scaled, 1)
                pool.wait_ge(pool_wp_scaled, h + 1)
                pool.nop(nofuse=True)
                pool.tensor_copy(wp_hi[:, par], wp_raw[:, par]).then_inc(pool_wp_hi, 1)
                pool.wait_ge(pool_wp_hi, h + 1)
                pool.tensor_tensor(wp_lo[:, par], wp_raw[:, par], wp_hi[:, par].bitcast(f32),
                                   ALU.subtract).then_inc(wp_split, 1)

            def norm_qk(h, k):
                n = NPAIR * h + k
                pool.wait_ge(qk_meansq, n + 1)
                pool.tensor_tensor(qk_r[:, k % 2, :], qk_ms[:, k % 2, :], minus_half[:, 0:4],
                                   ALU.pow).then_inc(pool_r, 1)
                pool.wait_ge(pool_r, n + 1)
                past(pool, qkT_ready, n - 1)
                pool.tensor_tensor(
                    qk_n[:, k % 2], stage[:, k % 2, :, 0:2 * D].rearrange("p t (a d) -> p t a d", d=D),
                    qk_r[:, k % 2, :].rearrange("p (t a) -> p t a", a=2).unsqueeze(3).broadcast_to([P, 2, 2, D]),
                    ALU.mult).then_inc(qk_normed, 1)

            def norm_y(h, g, now):
                pool.wait_ge(misc_read, misc_done(now, f"ss{g}"))
                pool.tensor_tensor(y_r[:, g, :], y_ms[:, g, :], minus_half[:, 0:4], ALU.pow).then_inc(y_normed, 1)

            pool.wait_ge(small_loaded, 80)
            split_w(0, 0)
            for k in range(NPAIR):
                norm_qk(0, k)
                if k == 0:
                    split_w(1, 1)

            def head(h, par):
                last = is_last(h)
                if not (isinstance(h, int) and h + 2 >= H):
                    split_w(h + 2, par)
                if not last:
                    norm_qk(h + 1, 0)
                    norm_qk(h + 1, 1)
                if not (isinstance(h, int) and h == 0):
                    norm_y(h - 1, 1, h)
                if not last:
                    norm_qk(h + 1, 2)
                    norm_qk(h + 1, 3)
                split_wp(h, par)
                norm_y(h, 0, h)

            over_heads(pool, head)
            norm_y(H - 1, 1, H)

        @block.tensor
        def _(pe):
            def product(dst, a_hi, a_lo, b_hi, b_lo, start=True, stop=True):
                pe.matmul(dst, a_hi, b_hi, start=start, stop=False)
                pe.matmul(dst, a_hi, b_lo, start=False, stop=False)
                return pe.matmul(dst, a_lo, b_hi, start=False, stop=stop)

            def misc_free(h, job):
                past(pe, misc_read, misc_done(h, job) - 1)

            def project(h, par, k):
                if k == 0:
                    pe.wait_ge(w_split, h + 1)
                past(pe, qkv_read, NT * h + k)
                for kt in range(KT):
                    at = (slice(None), kt, slice(k * P, (k + 1) * P))
                    last = product(qkv_ps[:, 0:3 * D], xT_hi[at], xT_lo[at], w_hi[:, par, kt], w_lo[:, par, kt],
                                   start=kt == 0, stop=kt == KT - 1)
                last.then_inc(qkv_ready, 1)

            def transpose_qk(h, par, k, now):
                misc_free(now, f"qkT{k}")
                pe.wait_ge(qk_normed, NPAIR * h + k + 1)
                for a in range(2):
                    for t in range(2):
                        last = pe.transpose(misc[:, (2 * a + t) * P:(2 * a + t + 1) * P],
                                            qk_n[:, k % 2, t, a, :], ident[:, :])
                last.then_inc(qkT_ready, 1)

            def score(h, par, s):
                i, n = ORDER[s], NT * h + s
                if s == 0:
                    pe.wait_ge(misc_read, misc_done(h - 1, "qkT3"))
                past(pe, scores_masked, n - 1)
                ps, at, parts = score_at(i)
                q = (slice(None), par, slice(i * P, (i + 1) * P))
                for a, b in parts:
                    last = product(ps[:, at + a:at + b], qT_hi[q], qT_lo[q], kT_hi[:, par, a:b], kT_lo[:, par, a:b])
                last.then_inc(scores_ready, 1)

            def transpose_probs(h, s):
                pe.wait_ge(probs_ready, NT * h + s + 1)
                for k, (a, b) in enumerate(CHUNKS[s]):
                    c = CPH * h + CHUNK0[s] + k
                    ps = pT_ps[(CHUNK0[s] + k) % 2]
                    past(pe, pT_split, c - 1)
                    for j in range(a, b):
                        last = pe.transpose(ps[:, (j - a) * P:(j - a + 1) * P],
                                            probs[:, s % 2, j * P:(j + 1) * P], ident[:, :])
                    last.then_inc(pT_ready, 1)

            def attend(h, par, g, half):
                nj = GROUPS[g][0] + 1
                weight = [sum(i >= j for i in GROUPS[g]) for j in range(nj)]
                cut = next(j for j in range(nj + 1) if 2 * sum(weight[:j]) >= sum(weight))
                if half == 0:
                    pe.wait_ge(pT_split, CPH * h + CHUNK0[4 * (g + 1)])
                    pe.wait_ge(v_split, NPAIR * (h + 1))
                    past(pe, y_split, 2 * h + g)
                for j in range(0, cut) if half == 0 else range(cut, nj):
                    w = weight[j] * P
                    last = product(yT_ps[:, 0:w], v_hi[:, par, j, :], v_lo[:, par, j, :],
                                   pT_hi[g][:, j, 0:w], pT_lo[g][:, j, 0:w], start=j == 0, stop=j == nj - 1)
                if half == 1:
                    last.then_inc(yT_ready, 1)

            def sum_squares(h, g, now):
                misc_free(now, f"ss{g}")
                pe.wait_ge(y_squared, 2 * h + g + 1)
                for r in range(4):
                    last = pe.matmul(misc[:, r:r + 1], y_sq[:, g, r * P:(r + 1) * P], ones[:, 0:1],
                                     start=True, stop=True)
                last.then_inc(ss_ready, 1)

            def project_out(h, par, g, half, now):
                misc_free(now, f"proj{g}{'ab'[half]}")
                if half == 0:
                    pe.wait_ge(y_split, 2 * h + g + 1)
                    pe.wait_ge(wp_split, h + 1)
                for r in (2 * half, 2 * half + 1):
                    at = (slice(None), g, slice(r * P, (r + 1) * P))
                    last = product(misc[:, (r % 2) * C:(r % 2 + 1) * C], yT_hi[at], yT_lo[at],
                                   wp_hi[:, par], wp_lo[:, par])
                last.then_inc(proj_ready, 1)

            pe.wait_ge(const_ready, 2)
            for n in range(2 * KT):
                half, kt = n // KT, n % KT
                pe.wait_ge(xn_ready, 4 * half + 4)
                past(pe, xT_read, n - 1)
                for t in range(4):
                    last = pe.transpose(pT_ps[n % 2][:, t * P:(t + 1) * P],
                                        bias_xn(4 * half + t)[:, kt * P:(kt + 1) * P], ident[:, :])
                last.then_inc(xT_ready, 1)
            pe.wait_ge(xT_read, 2 * KT)
            for k in range(NT):
                project(0, 0, k)
                if k % 2 and k >= 3:
                    transpose_qk(0, 0, k // 2 - 1, -1)
            pe.wait_ge(wb_ready, 1)
            w8T_ps = pT_ps[0][:, :].bitcast(bf16)
            for o in range(KT):
                for i in range(KT):
                    last = pe.transpose(w8T_ps[:, (i * KT + o) * P:(i * KT + o + 1) * P],
                                        wb[:, o, i * P:(i + 1) * P], ident_b[:, :])
            last.then_inc(w8T_ready, 1)
            transpose_qk(0, 0, NPAIR - 1, -1)
            pe.wait_ge(w8T_read, 1)
            pe.wait_ge(xq_ready, 1)
            for n in range(NT // 2):
                past(pe, ffn_added, n - 1)
                for t in (2 * n, 2 * n + 1):
                    for kt in range(KT):
                        last = pe.matmul(pT_ps[n % 2][:, (t % 2) * C:(t % 2 + 1) * C], xqT[:, kt, t * P:(t + 1) * P],
                                         w8T[:, kt, :], start=kt == 0, stop=kt == KT - 1)
                last.then_inc(ffn_ready, 1)
            score(0, 0, 0)
            pe.wait_ge(ffn_added, NT // 2)

            def head(h, par):
                first, last = isinstance(h, int) and h == 0, is_last(h)
                for s in range(NT):
                    if s < NT - 1:
                        score(h, par, s + 1)
                    elif not last:
                        score(h + 1, 1 - par, 0)
                    if s == 0:
                        if not last:
                            project(h + 1, 1 - par, 0)
                        if not first:
                            attend(h - 1, 1 - par, 1, 0)
                    if s == 1:
                        if not last:
                            project(h + 1, 1 - par, 1)
                        if not first:
                            attend(h - 1, 1 - par, 1, 1)
                    if s in (2, 3, 4) and not last:
                        project(h + 1, 1 - par, 2 * s - 2)
                    if s == 3 and not first:
                        sum_squares(h - 1, 1, h)
                    if s in (2, 3, 4) and not last:
                        project(h + 1, 1 - par, 2 * s - 1)
                    if s == 5:
                        if not first:
                            project_out(h - 1, 1 - par, 1, 0, h)
                        attend(h, par, 0, 0)
                    if s in (2, 3, 4, 5) and not last:
                        transpose_qk(h + 1, 1 - par, s - 2, h)
                    if s == 6:
                        if not first:
                            project_out(h - 1, 1 - par, 1, 1, h)
                        attend(h, par, 0, 1)
                    if s == 7:
                        sum_squares(h, 0, h)
                        project_out(h, par, 0, 0, h)
                    transpose_probs(h, s)
                    if s == 7:
                        project_out(h, par, 0, 1, h)

            over_heads(pe, head)
            attend(H - 1, 1, 1, 0)
            attend(H - 1, 1, 1, 1)
            sum_squares(H - 1, 1, H)
            project_out(H - 1, 1, 1, 0, H)
            project_out(H - 1, 1, 1, 1, H)

        @block.scalar
        def _(act):
            def copy_qkv(h, k):
                n, pair = NT * h + k, NPAIR * h + k // 2
                act.wait_ge(qkv_ready, n + 1)
                if k % 2 == 0:
                    past(act, v_split, pair - 1)
                    past(act, qk_normed, pair - 1)
                act.activation(stage[:, (k // 2) % 2, k % 2, :], qkv_ps[:, 0:3 * D], ACT.Copy).then_inc(qkv_read, 1)

            def square_qk(h, k):
                n = NPAIR * h + k
                act.wait_ge(qkv_read, 2 * n + 2)
                past(act, qk_meansq, n)
                act.activation(squares[:, :, :], stage[:, k % 2, :, 0:2 * D], ACT.Square).then_inc(qk_squared, 1)

            def qk_hi(h, par, k):
                act.wait_ge(qkT_ready, NPAIR * h + k + 1)
                at = slice(2 * k * P, (2 * k + 2) * P)
                act.activation(qT_hi[:, par, at], misc[:, 0:2 * P], ACT.Copy, scale=q_col[:, 2:3])
                act.activation(kT_hi[:, par, at], misc[:, 2 * P:4 * P], ACT.Copy).then_inc(qkT_hi_done, 1)

            def exps(h, par, s):
                i, n = ORDER[s], NT * h + s
                g, r = RANK[i]
                act.wait_ge(scores_masked, n + 1)
                act.activation(probs[:, s % 2, 0:(i + 1) * P], probs[:, s % 2, 0:(i + 1) * P], ACT.Exp,
                               bias=neg_max[:, par, s:s + 1], scale=-1.0,
                               accum_out=row_sum[:, par, g, r:r + 1]).then_inc(probs_ready, 1)

            def probs_hi(h, s):
                g, r = RANK[ORDER[s]]
                for k, (a, b) in enumerate(CHUNKS[s]):
                    act.wait_ge(pT_ready, CPH * h + CHUNK0[s] + k + 1)
                    act.activation(pT_hi[g][:, a:b, r * P:(r + 1) * P],
                                   pT_ps[(CHUNK0[s] + k) % 2][:, 0:(b - a) * P].rearrange("p (j t) -> p j t", t=P),
                                   ACT.Copy).then_inc(pT_hi_done, 1)

            def y_out(h, g):
                act.wait_ge(yT_ready, 2 * h + g + 1)
                act.activation(yT_hi[:, g, :], yT_ps[:, :], ACT.Copy).then_inc(y_hi_done, 1)
                act.activation(y_sq[:, g, :], yT_ps[:, :], ACT.Square).then_inc(y_squared, 1)

            def make_bias(h, par):
                past(act, scores_masked, NT * (h - 1))
                act.activation(bias[:, par, :], dist[:, :], ACT.Copy, scale=slopes[:, bass.ds(h, 1)]
                               ).then_inc(bias_ready, 1)

            for n in range(2 * KT):
                half, kt = n // KT, n % KT
                act.wait_ge(xT_ready, n + 1)
                act.activation(xT_hi[:, kt, half * 512:(half + 1) * 512], pT_ps[n % 2][:, :],
                               ACT.Copy).then_inc(xT_hi_done, 1)
            for k in range(NT):
                copy_qkv(0, k)
                if k % 2:
                    square_qk(0, k // 2)
                if k % 2 and k >= 3:
                    if k == 3:
                        act.wait_ge(small_loaded, 80)
                        act.wait_ge(wq_col_ready, 1)
                    qk_hi(0, 0, k // 2 - 1)
            act.wait_ge(w8T_ready, 1)
            act.activation(w8T[:, :, :].rearrange("p k o -> p (k o)"), pT_ps[0][:, :].bitcast(bf16)[:, 0:KT * C],
                           ACT.Copy).then_inc(w8T_read, 1)
            qk_hi(0, 0, NPAIR - 1)
            act.wait_ge(const_ready, 3)
            act.wait_ge(xq_ready, 1)
            make_bias(0, 0)
            make_bias(1, 1)
            exps(0, 0, 0)

            def head(h, par):
                first, last = isinstance(h, int) and h == 0, is_last(h)
                for s in range(NT):
                    if s > 0:
                        probs_hi(h, s - 1)
                    elif not first:
                        probs_hi(h - 1, NT - 1)
                    if s in (3, 4, 5, 6) and not last:
                        qk_hi(h + 1, 1 - par, s - 3)
                    if s == 2 and not first:
                        y_out(h - 1, 1)
                    if s < 5 and not last:
                        copy_qkv(h + 1, [0, 1, 2, 4, 6][s])
                    if s == 1 and not last:
                        square_qk(h + 1, 0)
                    if s == 7:
                        y_out(h, 0)
                    if s < NT - 1:
                        exps(h, par, s + 1)
                    elif not last:
                        exps(h + 1, 1 - par, 0)
                    if s in (2, 3, 4) and not last:
                        copy_qkv(h + 1, 2 * s - 1)
                        square_qk(h + 1, s - 1)
                    if s == 7 and not (isinstance(h, int) and h + 2 >= H):
                        make_bias(h + 2, par)

            over_heads(act, head)
            probs_hi(H - 1, NT - 1)
            y_out(H - 1, 1)

        @block.vector
        def _(dve):
            steps = [0]

            def link(ins):
                steps[0] += 1
                ins.then_inc(dve_step, 1)
                dve.wait_ge(dve_step, steps[0])

            def mean_squares(h, k):
                n = NPAIR * h + k
                dve.wait_ge(qk_squared, n + 1)
                past(dve, qk_normed, n - 1)
                dve.tensor_reduce(qk_ms[:, k % 2, :], squares[:, :, :].rearrange("p t (a d) -> p (t a) d", d=D),
                                  AX.X, ALU.add).then_inc(qk_summed, 1)
                dve.wait_ge(qk_summed, n + 1)
                dve.tensor_scalar(qk_ms[:, k % 2, :], qk_ms[:, k % 2, :], 1.0 / D, EPS,
                                  ALU.mult, ALU.add).then_inc(qk_meansq, 1)

            def split_v(h, par, k):
                n = NPAIR * h + k
                dve.wait_ge(qkv_read, 2 * n + 2)
                past(dve, yT_ready, 2 * (h - 1))
                v = stage[:, k % 2, :, 2 * D:3 * D]
                dve.tensor_copy(v_hi[:, par, 2 * k:2 * k + 2, :], v).then_inc(v_hi_done, 1)
                dve.wait_ge(v_hi_done, n + 1)
                dve.tensor_tensor(v_lo[:, par, 2 * k:2 * k + 2, :], v, v_hi[:, par, 2 * k:2 * k + 2, :].bitcast(f32),
                                  ALU.subtract).then_inc(v_split, 1)

            def qk_lo(h, par, k):
                dve.wait_ge(qkT_hi_done, NPAIR * h + k + 1)
                at = slice(2 * k * P, (2 * k + 2) * P)
                dve.scalar_tensor_tensor(qT_lo[:, par, at], misc[:, 0:2 * P], q_col[:, 2:3],
                                         qT_hi[:, par, at].bitcast(f32), ALU.mult, ALU.subtract)
                dve.tensor_tensor(kT_lo[:, par, at], misc[:, 2 * P:4 * P], kT_hi[:, par, at].bitcast(f32),
                                  ALU.subtract).then_inc(misc_read, 1)

            def mask(h, par, s):
                i, n = ORDER[s], NT * h + s
                ps, at, _ = score_at(i)
                w = (i + 1) * P
                dve.wait_ge(scores_ready, n + 1)
                if s == 0:
                    dve.wait_ge(bias_ready, h + 1)
                s2, h2 = (s - 2, h) if s >= 2 else (s - 2 + NT, h - 1)
                past(dve, pT_ready, CPH * h2 + CHUNK0[s2 + 1])
                dve.nop(nofuse=True)
                dve.tensor_tensor_reduce(out=probs[:, s % 2, 0:w], in0=ps[:, at:at + w],
                                         in1=bias[:, par, (NT - 1 - i) * P:(NT - 1 - i) * P + w],
                                         scale=1.0, scalar=3.0e38, op0=ALU.add, op1=ALU.min,
                                         accum_out=neg_max[:, par, s:s + 1]).then_inc(scores_masked, 1)

            def probs_lo(h, s):
                g, r = RANK[ORDER[s]]
                for k, (a, b) in enumerate(CHUNKS[s]):
                    dve.wait_ge(pT_hi_done, CPH * h + CHUNK0[s] + k + 1)
                    dve.tensor_tensor(pT_lo[g][:, a:b, r * P:(r + 1) * P],
                                      pT_ps[(CHUNK0[s] + k) % 2][:, 0:(b - a) * P].rearrange("p (j t) -> p j t", t=P),
                                      pT_hi[g][:, a:b, r * P:(r + 1) * P].bitcast(f32),
                                      ALU.subtract).then_inc(pT_split, 1)

            def y_lo(h, g):
                dve.wait_ge(y_squared, 2 * h + g + 1)
                dve.tensor_tensor(yT_lo[:, g, :], yT_ps[:, :], yT_hi[:, g, :].bitcast(f32),
                                  ALU.subtract).then_inc(y_split, 1)

            def y_mean(h, par, g):
                dve.scalar_tensor_tensor(y_el2[:, g, :], row_sum[:, par, g, :], EPS, row_sum[:, par, g, :],
                                         ALU.mult, ALU.mult).then_inc(el2_ready, 1)
                dve.wait_ge(el2_ready, 2 * h + g + 1)
                dve.wait_ge(ss_ready, 2 * h + g + 1)
                dve.scalar_tensor_tensor(y_ms[:, g, :], misc[:, 0:4], 1.0 / D, y_el2[:, g, :],
                                         ALU.mult, ALU.add).then_inc(misc_read, 1)

            def add_out(h, g, half):
                dve.wait_ge(proj_ready, 4 * h + 2 * g + half + 1)
                dve.wait_ge(y_normed, 2 * h + g + 1)
                for r in (2 * half, 2 * half + 1):
                    t = GROUPS[g][r]
                    last = dve.scalar_tensor_tensor(acc[:, t, :], misc[:, (r % 2) * C:(r % 2 + 1) * C],
                                                    y_r[:, g, r:r + 1], acc[:, t, :], ALU.mult, ALU.add)
                last.then_inc(misc_read, 1)

            for t in range(NT):
                if t % 2 == 0:
                    dve.wait_ge(x_loaded, 16 * NT // 2)
                last = dve.bn_stats(stats[:, t, :], acc[:, t, :])
            link(last)
            for t in range(NT):
                last = dve.bn_aggr(mean_var[:, t, :], stats[:, t, :])
            link(last)
            dve.tensor_scalar(rstd[:, :], mean_var[:, :, 1], EPS, None, ALU.add).then_inc(var_ready, 1)
            dve.wait_ge(rstd_ready, 1)
            for t in range(NT):
                dve.tensor_scalar(bias_xn(t), acc[:, t, :], mean_var[:, t, 0:1], rstd[:, t:t + 1],
                                  ALU.subtract, ALU.mult).then_inc(xn_ready, 1)
            dve.wait_ge(small_loaded, 80)
            dve.scalar_tensor_tensor(q_col[:, 2:3], q_col[:, 0:1], -SCALE, q_col[:, 1:2],
                                     ALU.mult, ALU.mult).then_inc(wq_col_ready, 1)
            link(dve.tensor_copy(ffn_s[:, 0:1], xs_b[:, :]))
            link(dve.reciprocal(ffn_s[:, 1:2], ffn_s[:, 0:1]))
            dve.tensor_tensor(ffn_s[:, 3:4], ffn_s[:, 0:1], ffn_s[:, 2:3], ALU.mult)
            u = probs[:, :, :].rearrange("p a t -> p (a t)")
            for n in range(2 * KT):
                half, kt = n // KT, n % KT
                at = slice(half * 512, (half + 1) * 512)
                dve.wait_ge(xT_hi_done, n + 1)
                dve.tensor_scalar(u[:, kt * T + half * 512:kt * T + (half + 1) * 512], pT_ps[n % 2][:, :],
                                  ffn_s[:, 1:2], E4M3_MAX, ALU.mult, ALU.min)
                dve.tensor_tensor(xT_lo[:, kt, at], pT_ps[n % 2][:, :], xT_hi[:, kt, at].bitcast(f32),
                                  ALU.subtract).then_inc(xT_read, 1)
            mean_squares(0, 0)
            split_v(0, 0, 0)
            m = bias[:, :, :].rearrange("p a t -> p (a t)")
            link(dve.tensor_scalar(u, u, -E4M3_MAX, None, ALU.max))
            link(dve.tensor_scalar(m.bitcast(i32), u.bitcast(i32), 0x7F800000, None, ALU.bitwise_and))
            mean_squares(0, 1)
            split_v(0, 0, 1)
            qk_lo(0, 0, 0)
            link(dve.tensor_scalar(m, m, 2.0 ** -6, 1.5 * 2.0 ** 20, ALU.max, ALU.mult))
            link(dve.tensor_tensor(u, u, m, ALU.add))
            mean_squares(0, 2)
            split_v(0, 0, 2)
            qk_lo(0, 0, 1)
            dve.tensor_tensor(xqT[:, :, :].rearrange("p k t -> p (k t)"), u, m, ALU.subtract).then_inc(xq_ready, 1)
            mean_squares(0, 3)
            split_v(0, 0, 3)
            qk_lo(0, 0, 2)
            dve.wait_ge(w8_loaded, 16)
            dve.wait_ge(xq_ready, 1)
            code = u[:, 0:KT * C].bitcast(i32)
            mag = u[:, KT * C:2 * KT * C]
            alt = u[:, 2 * KT * C:3 * KT * C]
            sign = u[:, 3 * KT * C:4 * KT * C]
            link(dve.tensor_copy(code, w8[:, :, :].rearrange("p k i -> p (k i)")))
            dve.tensor_scalar(sign, code, 128, -2.0, ALU.is_ge, ALU.mult)
            link(dve.tensor_scalar(mag.bitcast(i32), code, 0x7F, 20, ALU.bitwise_and, ALU.logical_shift_left))
            link(dve.tensor_scalar(mag.bitcast(i32), mag.bitcast(i32), 112 << 23, None, ALU.bitwise_or))
            link(dve.tensor_scalar(mag, mag, 256.0, None, ALU.mult))
            link(dve.tensor_scalar(alt, mag, 2.0, -(2.0 ** -6), ALU.mult, ALU.add))
            link(dve.tensor_tensor(mag, mag, alt, ALU.min))
            dve.scalar_tensor_tensor(wb[:, :, :].rearrange("p k i -> p (k i)"), sign, 1.0, mag,
                                     ALU.add, ALU.mult).then_inc(wb_ready, 1)
            qk_lo(0, 0, NPAIR - 1)
            for n in range(NT // 2):
                dve.wait_ge(ffn_ready, n + 1)
                for t in (2 * n, 2 * n + 1):
                    last = dve.scalar_tensor_tensor(acc[:, t, :], pT_ps[n % 2][:, (t % 2) * C:(t % 2 + 1) * C],
                                                    ffn_s[:, 3:4], acc[:, t, :], ALU.mult, ALU.add)
                last.then_inc(ffn_added, 1)
            mask(0, 0, 0)

            def head(h, par):
                first, last = isinstance(h, int) and h == 0, is_last(h)
                for s in range(NT):
                    if s > 0:
                        probs_lo(h, s - 1)
                    elif not first:
                        probs_lo(h - 1, NT - 1)
                    if s in (2, 3, 4, 5) and not last:
                        mean_squares(h + 1, s - 2)
                    if s in (3, 4, 5, 6) and not last:
                        qk_lo(h + 1, 1 - par, s - 3)
                    if s < NT - 1:
                        mask(h, par, s + 1)
                    elif not last:
                        mask(h + 1, 1 - par, 0)
                    if s == 2 and not first:
                        y_lo(h - 1, 1)
                    if s == 3 and not first:
                        y_mean(h - 1, 1 - par, 1)
                    if s in (2, 3, 4, 5) and not last:
                        split_v(h + 1, 1 - par, s - 2)
                    if s == 5 and not first:
                        add_out(h - 1, 1, 0)
                    if s == 6 and not first:
                        add_out(h - 1, 1, 1)
                    if s == 7:
                        y_lo(h, 0)
                        y_mean(h, par, 0)
                        add_out(h, 0, 0)
                        add_out(h, 0, 1)

            over_heads(dve, head)
            probs_lo(H - 1, NT - 1)
            y_lo(H - 1, 1)
            y_mean(H - 1, 1, 1)
            add_out(H - 1, 1, 0)
            add_out(H - 1, 1, 1)


def kernel(L0_attn_x, L0_attn_Wq, L0_attn_Wk, L0_attn_Wv, L0_attn_Wproj, L0_attn_q_rms_w, L0_attn_k_rms_w,
           L0_attn_subln_w, L0_ffn_weight, L0_ffn_weight_scale, L0_ffn_input_scale):
    import concourse.bacc as bacc
    from concourse.bass_utils import run_bass_kernel_spmd

    nc = bacc.Bacc("TRN2", target_bir_lowering=False, num_devices=1)
    shaped = {
        "x": np.asarray(L0_attn_x)[0],
        "wq": L0_attn_Wq, "wk": L0_attn_Wk, "wv": L0_attn_Wv, "wproj": L0_attn_Wproj,
        "q_w": np.asarray(L0_attn_q_rms_w).reshape(-1, 1),
        "k_w": np.asarray(L0_attn_k_rms_w).reshape(-1, 1),
        "sub_w": np.asarray(L0_attn_subln_w).reshape(-1, 1),
        "ffn_w": np.asarray(L0_ffn_weight).view(np.uint8),
        "ffn_ws": np.asarray(L0_ffn_weight_scale).reshape(1, 1),
        "ffn_xs": np.asarray(L0_ffn_input_scale).reshape(1, 1),
    }
    arrays, aps = {}, {}
    for name, a in shaped.items():
        a = np.ascontiguousarray(a)
        arrays["in_" + name] = a
        aps[name] = nc.dram_tensor("in_" + name, a.shape, mybir.dt.from_np(a.dtype), kind="ExternalInput").ap()
    rows, cols = shaped["x"].shape
    out = nc.dram_tensor("out", (rows, cols), mybir.dt.float32, kind="ExternalOutput").ap()
    build_block(nc, out=out, **aps)
    got = run_bass_kernel_spmd(nc, [arrays], core_ids=[0])
    return got.results[0]["out"].reshape(1, rows, cols)
```

```python
import numpy as np
import concourse.bass as bass
from concourse import mybir
from contextlib import ExitStack



def build_block(nc, x, wq, wk, wv, wproj, q_w, k_w, sub_w, ffn_w, ffn_ws, ffn_xs, out):
    f32, f32r, bf16 = mybir.dt.float32, mybir.dt.float32r, mybir.dt.bfloat16
    i32, u8 = mybir.dt.int32, mybir.dt.uint8
    ALU, ACT, AX = mybir.AluOpType, mybir.ActivationFunctionType, mybir.AxisListType

    P = 128
    T, C = x.shape[0], x.shape[1]
    D = q_w.shape[0]
    H = wq.shape[1] // D
    NT = T // P
    KT = C // P
    NPAIR = NT // 2
    EPS = 1e-5
    SCALE = float(D) ** -0.5
    BIG = 1e30
    E4M3_MAX = 448.0

    ORDER = [7, 0, 6, 1, 5, 2, 4, 3]
    GROUPS = [sorted(ORDER[:4], reverse=True), sorted(ORDER[4:], reverse=True)]
    RANK = {i: (g, GROUPS[g].index(i)) for g in range(2) for i in GROUPS[g]}
    CHUNKS = [[(j, min(j + 4, i + 1)) for j in range(0, i + 1, 4)] for i in ORDER]
    CHUNK0 = [sum(len(c) for c in CHUNKS[:s]) for s in range(NT + 1)]
    CPH = CHUNK0[NT]

    MISC = ["ss0", "proj0a", "proj0b", "qkT0", "ss1", "qkT1", "qkT2", "qkT3", "proj1a", "proj1b"]
    JOB_BANK = {"ss0": "qkv", "proj0b": "yT", "ss1": "yT", "qkT2": "qkv", "proj1a": "qkv"}
    MISC_FIRST = [m for m in MISC if m.startswith("qkT")]
    MISC_LAST = [m for m in MISC if not m.startswith("qkT")]
    MISC_TAIL = ["ss0", "proj0a", "proj0b", "ss1", "proj1a", "proj1b"]

    def misc_done(h, job):
        if isinstance(h, int) and h < 0:
            return int(job[3]) + 1
        if isinstance(h, int) and h == 0:
            return NPAIR + MISC_FIRST.index(job) + 1
        base = NPAIR + len(MISC_FIRST) + (h - 1) * len(MISC)
        if isinstance(h, int) and h == H - 1:
            return base + MISC_LAST.index(job) + 1
        if isinstance(h, int) and h == H:
            return base - len(MISC) + len(MISC_LAST) + MISC_TAIL.index(job) + 1
        return base + MISC.index(job) + 1

    def past(eng, sem, count):
        if not isinstance(count, int) or count > 0:
            eng.wait_ge(sem, count)

    ctx = ExitStack()
    with ctx:
        def sb(name, shape, dt=f32):
            return ctx.enter_context(nc.sbuf_tensor(name, shape, dt))

        def pb(name, shape, dt=f32):
            return ctx.enter_context(nc.psum_tensor(name, shape, dt))

        def sem(name):
            return ctx.enter_context(nc.semaphore(name))

        ident = sb("ident", [P, P])
        ident_b = sb("ident_b", [P, P], bf16)
        ones = sb("ones", [P, 1])
        minus_half = sb("minus_half", [P, NT])
        slopes = sb("slopes", [P, H])
        dist = sb("dist", [P, T])
        acc = sb("acc", [P, NT, C])
        xT_hi = sb("xT_hi", [P, KT, T], f32r)
        xT_lo = sb("xT_lo", [P, KT, T], f32r)
        w_raw = sb("w_raw", [P, 2, KT, 3 * D])
        w_hi = sb("w_hi", [P, 2, KT, 3 * D], f32r)
        w_lo = sb("w_lo", [P, 2, KT, 3 * D], f32r)
        wp_raw = sb("wp_raw", [P, 2, C])
        wp_hi = sb("wp_hi", [P, 2, C], f32r)
        wp_lo = sb("wp_lo", [P, 2, C], f32r)
        stage = sb("stage", [P, 2, 2, 3 * D])
        squares = sb("squares", [P, 2, 2 * D])
        qk_ms = sb("qk_ms", [P, 2, 4])
        qk_r = sb("qk_r", [P, 2, 4])
        qk_n = sb("qk_n", [P, 2, 2, 2, D])
        qT_hi = sb("qT_hi", [P, 2, T], f32r)
        qT_lo = sb("qT_lo", [P, 2, T], f32r)
        kT_hi = sb("kT_hi", [P, 2, T], f32r)
        kT_lo = sb("kT_lo", [P, 2, T], f32r)
        v_hi = sb("v_hi", [P, 2, NT, D], f32r)
        v_lo = sb("v_lo", [P, 2, NT, D], f32r)
        bias = sb("bias", [P, 2, T])
        probs = sb("probs", [P, 2, T])
        neg_max = sb("neg_max", [P, 2, NT])
        row_sum = sb("row_sum", [P, 2, 2, 4])
        pT_hi = [sb(f"pT_hi{g}", [P, GROUPS[g][0] + 1, 4 * P], f32r) for g in range(2)]
        pT_lo = [sb(f"pT_lo{g}", [P, GROUPS[g][0] + 1, 4 * P], f32r) for g in range(2)]
        yT_hi = sb("yT_hi", [P, 2, 4 * P], f32r)
        yT_lo = sb("yT_lo", [P, 2, 4 * P], f32r)
        y_sq = sb("y_sq", [P, 2, 4 * P])
        y_ms = sb("y_ms", [P, 2, 4])
        y_el2 = sb("y_el2", [P, 2, 4])
        y_r = sb("y_r", [P, 2, 4])
        q_col = sb("q_col", [P, 4])
        stats = sb("stats", [P, NT, 6])
        mean_var = sb("mean_var", [P, NT, 2])
        rstd = sb("rstd", [P, NT])
        xs_b = sb("xs_b", [P, 1], bf16)
        ffn_s = sb("ffn_s", [P, 4])
        w8 = sb("w8", [P, KT, C], mybir.dt.from_np(np.dtype("uint8")))
        wb = sb("wb", [P, KT, C], bf16)
        w8T = sb("w8T", [P, KT, C], bf16)
        xqT = sb("xqT", [P, KT, T], bf16)

        score_big = pb("score_big", [P, 1024])
        score_small = pb("score_small", [P, 512])
        pT_ps = [pb(f"pT_ps{b}", [P, 512]) for b in range(2)]
        yT_ps = pb("yT_ps", [P, 512])
        qkv_ps = pb("qkv_ps", [P, 512])
        misc = pb("misc", [P, 512])

        x_loaded = [sem(f"x_loaded{n}") for n in range(2)]
        small_loaded = sem("small_loaded")
        w8_loaded = sem("w8_loaded")
        w_loaded = [sem(f"w_loaded{b}") for b in range(2)]
        wp_loaded = [sem(f"wp_loaded{b}") for b in range(2)]
        w_split = sem("w_split")
        wp_split = sem("wp_split")
        const_ready = sem("const_ready")
        pool_step = sem("pool_step")
        dve_step = sem("dve_step")
        xn_ready = sem("xn_ready")
        xT_ready = sem("xT_ready")
        xT_hi_done = sem("xT_hi_done")
        xT_read = sem("xT_read")
        var_ready = sem("var_ready")
        rstd_ready = sem("rstd_ready")
        wb_ready = sem("wb_ready")
        w8T_ready = sem("w8T_ready")
        w8T_read = sem("w8T_read")
        xq_ready = sem("xq_ready")
        ffn_ready = sem("ffn_ready")
        ffn_added = sem("ffn_added")
        qkv_ready = sem("qkv_ready")
        qkv_read = sem("qkv_read")
        qk_squared = sem("qk_squared")
        qk_meansq = sem("qk_meansq")
        qk_normed = sem("qk_normed")
        qk_summed = sem("qk_summed")
        qk_r_ready = sem("qk_r_ready")
        w_hi_done = sem("w_hi_done")
        wp_scaled = sem("wp_scaled")
        wp_hi_done = sem("wp_hi_done")
        wq_col_ready = sem("wq_col_ready")
        qkT_ready = sem("qkT_ready")
        qkT_hi_done = sem("qkT_hi_done")
        v_hi_done = sem("v_hi_done")
        v_split = sem("v_split")
        bias_ready = sem("bias_ready")
        scores_ready = sem("scores_ready")
        scores_masked = sem("scores_masked")
        probs_ready = sem("probs_ready")
        pT_ready = sem("pT_ready")
        pT_hi_done = sem("pT_hi_done")
        pT_split = sem("pT_split")
        yT_ready = sem("yT_ready")
        y_hi_done = sem("y_hi_done")
        y_squared = sem("y_squared")
        y_split = sem("y_split")
        ss_ready = sem("ss_ready")
        el2_ready = sem("el2_ready")
        y_normed = sem("y_normed")
        proj_ready = sem("proj_ready")
        misc_read = sem("misc_read")
        stored = sem("stored")

        block = ctx.enter_context(nc.Block())

        wq_v = wq.rearrange("(k p) (h d) -> p k h d", p=P, d=D)
        wk_v = wk.rearrange("(k p) (h d) -> p k h d", p=P, d=D)
        wv_v = wv.rearrange("(k p) (h d) -> p k h d", p=P, d=D)
        wp_v = wproj.rearrange("(h p) c -> p h c", p=P)
        x_v = x.rearrange("(t p) c -> p t c", p=P)
        out_v = out.rearrange("(t p) c -> p t c", p=P)

        def over_heads(eng, body):
            body(0, 0)
            body(1, 1)
            with eng.Fori(1, H // 2 - 1) as pair:
                body(pair * 2, 0)
                body(pair * 2 + 1, 1)
            body(H - 2, 0)
            body(H - 1, 1)

        w8T_ps = pT_ps[0][:, :].bitcast(bf16)

        def qkv_bank(h, k):
            return yT_ps if isinstance(h, int) and k % 2 and (h == 0 or h == 1 and k <= 5) else qkv_ps

        def first_ps(k):
            return score_small if k % 2 else misc

        def job_ps(job):
            return {"yT": yT_ps, "qkv": qkv_ps}.get(JOB_BANK.get(job), misc)

        QUANTIZE_AT = [(-1, 0), (-1, 1), (0, 0), (0, 1), (0, 2), (0, 3), (1, 0), (1, 1)]
        FFN_AT = [(0, 3), (0, 4), (1, 3), (1, 4)]

        def bias_xn(t):
            return bias[:, t // 4, (t % 4) * C:(t % 4 + 1) * C]

        def is_last(h):
            return isinstance(h, int) and h == H - 1

        def score_at(i):
            w = (i + 1) * P
            if i < 4:
                return score_small, 0, [(0, w)]
            if w == 640:
                return score_big, 128, [(0, 384), (384, 640)]
            return score_big, 0, [(0, 512), (512, w)]

        @block.sync
        def _(sp):
            for n in range(2):
                for t in range(n * NT // 2, (n + 1) * NT // 2, 2):
                    sp.dma_start(acc[:, t:t + 2, :], x_v[:, t:t + 2, :]).then_inc(x_loaded[n], 16)

            def load_w(h, par):
                for n, w in enumerate((wq_v, wk_v, wv_v)):
                    sp.dma_start(w_raw[:, par, :, n * D:(n + 1) * D], w[:, :, h, :]).then_inc(w_loaded[par], 16)

            def load_wp(h, par):
                sp.dma_start(wp_raw[:, par, :], wp_v[:, h, :]).then_inc(wp_loaded[par], 16)

            load_w(0, 0)
            load_w(1, 1)
            load_wp(0, 0)

            def head(h, par):
                if not (isinstance(h, int) and h + 2 >= H):
                    sp.wait_ge(w_split, h + 1)
                    load_w(h + 2, par)
                if not is_last(h):
                    past(sp, wp_split, h)
                    load_wp(h + 1, 1 - par)

            over_heads(sp, head)
            for g in range(2):
                sp.wait_ge(misc_read, misc_done(H, "proj0b") if g == 0 else misc_done(H, "proj1b"))
                for i in GROUPS[g]:
                    sp.dma_start(out_v[:, i, :], acc[:, i, :]).then_inc(stored, 16)
            sp.wait_ge(stored, 16 * NT)

        @block.gpsimd
        def _(pool):
            steps = [0]

            def link(ins):
                steps[0] += 1
                ins.then_inc(pool_step, 1)
                pool.wait_ge(pool_step, steps[0])

            pool.memset(minus_half[:, :], -0.5)
            link(pool.memset(ident[:, :], 0.0))
            pool.affine_select(out=ident[:, :], in_=ident[:, :], compare_op=ALU.not_equal, fill=1.0, base=0,
                               pattern=[[-1, P]], channel_multiplier=1).then_inc(const_ready, 1)
            pool.wait_ge(const_ready, 1)
            pool.tensor_copy(ident_b[:, :], ident[:, :]).then_inc(const_ready, 1)
            pool.memset(ones[:, :], 1.0)
            for h in range(H):
                pool.memset(slopes[:, h:h + 1], float(np.float32(2.0 ** (-0.5 * (h + 1)))))
            for n in range(2):
                at = slice(n * NT // 2, (n + 1) * NT // 2)
                pool.wait_ge(var_ready, n + 1)
                pool.tensor_tensor(rstd[:, at], rstd[:, at], minus_half[:, at], ALU.pow).then_inc(rstd_ready, 1)

            link(pool.iota(dist[:, :], pattern=[[-1, T]], base=T - P, channel_multiplier=1,
                           allow_small_or_imprecise_dtypes=True))
            pool.affine_select(out=dist[:, :], in_=dist[:, :], compare_op=ALU.is_ge, fill=BIG, base=T - P,
                               pattern=[[-1, T]], channel_multiplier=1).then_inc(const_ready, 1)

            def split_w(h, par):
                pool.wait_ge(w_loaded[par], 48 * (h // 2 + 1) if isinstance(h, int) else (h - par) * 24 + 48)
                past(pool, qkv_ready, (h - 1) * NT)
                pool.nop(nofuse=True)
                pool.tensor_copy(w_hi[:, par], w_raw[:, par]).then_inc(w_hi_done, 1)
                pool.wait_ge(w_hi_done, h + 1)
                pool.tensor_tensor(w_lo[:, par], w_raw[:, par], w_hi[:, par].bitcast(f32),
                                   ALU.subtract).then_inc(w_split, 1)

            def split_wp(h, par):
                pool.wait_ge(wp_loaded[par], 16 * (h // 2 + 1) if isinstance(h, int) else (h - par) * 8 + 16)
                past(pool, proj_ready, (h - 1) * 4)
                pool.nop(nofuse=True)
                pool.tensor_scalar(wp_raw[:, par], wp_raw[:, par], q_col[:, 3:4], None,
                                   ALU.mult).then_inc(wp_scaled, 1)
                pool.wait_ge(wp_scaled, h + 1)
                pool.nop(nofuse=True)
                pool.tensor_copy(wp_hi[:, par], wp_raw[:, par]).then_inc(wp_hi_done, 1)
                pool.wait_ge(wp_hi_done, h + 1)
                pool.tensor_tensor(wp_lo[:, par], wp_raw[:, par], wp_hi[:, par].bitcast(f32),
                                   ALU.subtract).then_inc(wp_split, 1)

            def norm_qk(h, k):
                n = NPAIR * h + k
                pool.wait_ge(qk_meansq, n + 1)
                pool.tensor_tensor(qk_r[:, k % 2, :], qk_ms[:, k % 2, :], minus_half[:, 0:4],
                                   ALU.pow).then_inc(qk_r_ready, 1)
                pool.wait_ge(qk_r_ready, n + 1)
                past(pool, qkT_ready, n - 1)
                pool.tensor_tensor(
                    qk_n[:, k % 2], stage[:, k % 2, :, 0:2 * D].rearrange("p t (a d) -> p t a d", d=D),
                    qk_r[:, k % 2, :].rearrange("p (t a) -> p t a", a=2).unsqueeze(3).broadcast_to([P, 2, 2, D]),
                    ALU.mult).then_inc(qk_normed, 1)

            def norm_y(h, g, now):
                pool.wait_ge(misc_read, misc_done(now, f"ss{g}"))
                pool.tensor_tensor(y_r[:, g, :], y_ms[:, g, :], minus_half[:, 0:4], ALU.pow).then_inc(y_normed, 1)

            for k in range(NPAIR):
                norm_qk(0, k)
            pool.wait_ge(small_loaded, 80)
            split_w(1, 1)

            def head(h, par):
                first, last = isinstance(h, int) and h == 0, is_last(h)
                if not first:
                    norm_y(h - 1, 0, h)
                if not (isinstance(h, int) and h + 2 >= H):
                    split_w(h + 2, par)
                if not last:
                    norm_qk(h + 1, 0)
                    norm_qk(h + 1, 1)
                    norm_qk(h + 1, 2)
                if not first:
                    norm_y(h - 1, 1, h)
                if not last:
                    norm_qk(h + 1, 3)
                split_wp(h, par)

            over_heads(pool, head)
            norm_y(H - 1, 0, H)
            norm_y(H - 1, 1, H)

        @block.tensor
        def _(pe):
            def product(dst, a_hi, a_lo, b_hi, b_lo, start=True, stop=True):
                pe.matmul(dst, a_hi, b_hi, start=start, stop=False)
                pe.matmul(dst, a_hi, b_lo, start=False, stop=False)
                return pe.matmul(dst, a_lo, b_hi, start=False, stop=stop)

            def bank_free(h, job):
                if isinstance(h, int) and h < 0:
                    past(pe, misc_read, misc_done(h, job) - 2)
                    return
                tail = isinstance(h, int) and h == H
                jobs = MISC_TAIL if tail else MISC_LAST if is_last(h) else MISC
                if isinstance(h, int) and h == 0:
                    jobs = MISC_FIRST
                bank = JOB_BANK.get(job)
                if job == "ss0":
                    pe.wait_ge(qkv_read, min(NT * (h + 1) + 1, NT * H) if isinstance(h, int) else NT * h + NT + 1)
                    pe.wait_ge(misc_read, misc_done(h - 1, "qkT2" if isinstance(h, int) and h == 1 else "proj1a"))
                    return
                same = [m for m in jobs[:jobs.index(job)] if JOB_BANK.get(m) == bank and m != "ss0"]
                if same:
                    pe.wait_ge(misc_read, misc_done(h, same[-1]))
                elif bank == "qkv":
                    pe.wait_ge(qkv_read, NT * (min(h + 2, H) if isinstance(h, int) else h + 2))
                elif bank == "yT":
                    pe.wait_ge(y_split, 2 * h)
                else:
                    before = "qkT3" if isinstance(h, int) and h <= 1 else "proj1b"
                    pe.wait_ge(misc_read, misc_done(h - 1, before))

            def project(h, par, k):
                if k == 0:
                    pe.wait_ge(w_split, h + 1)
                past(pe, qkv_read, NT * h + k - (1 if isinstance(h, int) and (h == 0 or h == 1 and 1 <= k <= 6) else 0))
                if k == 0 and not (isinstance(h, int) and h <= 1):
                    pe.wait_ge(misc_read, misc_done(h - 2, "proj1a" if not (isinstance(h, int) and h == 2) else "qkT2"))
                if k == 1 and not (isinstance(h, int) and h <= 1):
                    pe.wait_ge(misc_read, misc_done(h - 1, "ss0"))
                for kt in range(KT):
                    at = (slice(None), kt, slice(k * P, (k + 1) * P))
                    last = product(qkv_bank(h, k)[:, 0:3 * D], xT_hi[at], xT_lo[at], w_hi[:, par, kt], w_lo[:, par, kt],
                                   start=kt == 0, stop=kt == KT - 1)
                last.then_inc(qkv_ready, 1)

            def transpose_qk(h, par, k, now):
                bank_free(now, f"qkT{k}")
                pe.wait_ge(qk_normed, NPAIR * h + k + 1)
                ps = first_ps(k) if isinstance(now, int) and now < 0 else job_ps(f"qkT{k}")
                for a in range(2):
                    for t in range(2):
                        last = pe.transpose(ps[:, (2 * a + t) * P:(2 * a + t + 1) * P],
                                            qk_n[:, k % 2, t, a, :], ident[:, :])
                last.then_inc(qkT_ready, 1)

            def score(h, par, s):
                i, n = ORDER[s], NT * h + s
                if s == 0:
                    pe.wait_ge(misc_read, misc_done(h - 1, "qkT3"))
                past(pe, scores_masked, n - 1)
                ps, at, parts = score_at(i)
                q = (slice(None), par, slice(i * P, (i + 1) * P))
                for a, b in parts:
                    last = product(ps[:, at + a:at + b], qT_hi[q], qT_lo[q], kT_hi[:, par, a:b], kT_lo[:, par, a:b])
                last.then_inc(scores_ready, 1)

            def transpose_probs(h, s):
                pe.wait_ge(probs_ready, NT * h + s + 1)
                for k, (a, b) in enumerate(CHUNKS[s]):
                    c = CPH * h + CHUNK0[s] + k
                    ps = pT_ps[(CHUNK0[s] + k) % 2]
                    past(pe, pT_split, c - 1)
                    for j in range(a, b):
                        last = pe.transpose(ps[:, (j - a) * P:(j - a + 1) * P],
                                            probs[:, s % 2, j * P:(j + 1) * P], ident[:, :])
                    last.then_inc(pT_ready, 1)

            def attend(h, par, g, half):
                nj = GROUPS[g][0] + 1
                weight = [sum(i >= j for i in GROUPS[g]) for j in range(nj)]
                cut = next(j for j in range(nj + 1) if 2 * sum(weight[:j]) >= sum(weight))
                if half == 0:
                    pe.wait_ge(pT_split, CPH * h + CHUNK0[4 * (g + 1)])
                    pe.wait_ge(v_split, NPAIR * (h + 1))
                    past(pe, y_split, 2 * h + g)
                    if g == 0 and not (isinstance(h, int) and h == 0):
                        pe.wait_ge(misc_read, misc_done(h, "ss1"))
                    elif g == 0:
                        pe.wait_ge(ffn_added, NPAIR // 2)
                for j in range(0, cut) if half == 0 else range(cut, nj):
                    w = weight[j] * P
                    last = product(yT_ps[:, 0:w], v_hi[:, par, j, :], v_lo[:, par, j, :],
                                   pT_hi[g][:, j, 0:w], pT_lo[g][:, j, 0:w], start=j == 0, stop=j == nj - 1)
                if half == 1:
                    last.then_inc(yT_ready, 1)

            def sum_squares(h, g, now):
                bank_free(now, f"ss{g}")
                if isinstance(now, int) and now == 1 and g == 1:
                    pe.wait_ge(ffn_added, NPAIR)
                pe.wait_ge(y_squared, 2 * h + g + 1)
                for r in range(4):
                    last = pe.matmul(job_ps(f"ss{g}")[:, r:r + 1], y_sq[:, g, r * P:(r + 1) * P], ones[:, 0:1],
                                     start=True, stop=True)
                last.then_inc(ss_ready, 1)

            def project_out(h, par, g, half, now):
                bank_free(now, f"proj{g}{'ab'[half]}")
                if isinstance(now, int) and now == 1 and (g, half) == (0, 1):
                    pe.wait_ge(ffn_added, NPAIR - 1)
                if half == 0:
                    pe.wait_ge(y_split, 2 * h + g + 1)
                    pe.wait_ge(wp_split, h + 1)
                for r in (2 * half, 2 * half + 1):
                    at = (slice(None), g, slice(r * P, (r + 1) * P))
                    last = product(job_ps(f"proj{g}{'ab'[half]}")[:, (r % 2) * C:(r % 2 + 1) * C], yT_hi[at], yT_lo[at],
                                   wp_hi[:, par], wp_lo[:, par])
                last.then_inc(proj_ready, 1)

            pe.wait_ge(const_ready, 2)

            def transpose_x(n):
                half, kt = n // KT, n % KT
                pe.wait_ge(xn_ready, 4 * half + 4)
                past(pe, xT_read, n - 1)
                for t in range(4):
                    last = pe.transpose(pT_ps[n % 2][:, t * P:(t + 1) * P],
                                        bias_xn(4 * half + t)[:, kt * P:(kt + 1) * P], ident[:, :])
                last.then_inc(xT_ready, 1)

            for n in range(2 * KT):
                transpose_x(n)
            for k in range(NT):
                if k % 4 == 0:
                    pe.wait_ge(xT_read, KT * (k // 4 + 1))
                project(0, 0, k)
                if k == 3:
                    pe.wait_ge(wb_ready, 1)
                    for o in range(KT):
                        for i in range(KT):
                            last = pe.transpose(w8T_ps[:, (i * KT + o) * P:(i * KT + o + 1) * P],
                                                wb[:, o, i * P:(i + 1) * P], ident_b[:, :])
                    last.then_inc(w8T_ready, 1)
                if k == NT - 1:
                    transpose_qk(0, 0, 0, -1)
                    transpose_qk(0, 0, 1, -1)
            transpose_qk(0, 0, 2, -1)
            transpose_qk(0, 0, 3, -1)
            score(0, 0, 0)

            def ffn(n):
                if n == 0:
                    pe.wait_ge(w8T_read, 1)
                    pe.wait_ge(qkv_read, NT + 6)
                past(pe, ffn_added, n)
                pe.wait_ge(xq_ready, KT * (n + 1))
                if n >= NPAIR // 2:
                    pe.wait_ge(y_split, 2)
                    if n == NPAIR - 1:
                        pe.wait_ge(misc_read, misc_done(1, "proj0b"))
                for t in (2 * n, 2 * n + 1):
                    for kt in range(KT):
                        last = pe.matmul(yT_ps[:, (t % 2) * C:(t % 2 + 1) * C], xqT[:, kt, t * P:(t + 1) * P],
                                         w8T[:, kt, :], start=kt == 0, stop=kt == KT - 1)
                last.then_inc(ffn_ready, 1)

            def head(h, par):
                first, last = isinstance(h, int) and h == 0, is_last(h)
                for s in range(NT):
                    if s < NT - 1:
                        score(h, par, s + 1)
                    elif not last:
                        score(h + 1, 1 - par, 0)
                    if s == 0:
                        if not last:
                            project(h + 1, 1 - par, 0)
                        if not first:
                            attend(h - 1, 1 - par, 1, 0)
                            sum_squares(h - 1, 0, h)
                    if s == 1:
                        if not last:
                            project(h + 1, 1 - par, 1)
                        if not first:
                            attend(h - 1, 1 - par, 1, 1)
                    if isinstance(h, int) and h > 0 and (h, s) in FFN_AT:
                        ffn(FFN_AT.index((h, s)))
                    if s in (2, 3, 4):
                        if not last:
                            project(h + 1, 1 - par, 2 * s - 2)
                        if s == 4 and not first:
                            sum_squares(h - 1, 1, h)
                        elif not first:
                            project_out(h - 1, 1 - par, 0, s - 2, h)
                        if not last:
                            project(h + 1, 1 - par, 2 * s - 1)
                    if s in (3, 4) and not last:
                        transpose_qk(h + 1, 1 - par, s - 3, h)
                    if s == 5:
                        attend(h, par, 0, 0)
                        if not last:
                            transpose_qk(h + 1, 1 - par, 2, h)
                    if s == 6:
                        if not last:
                            transpose_qk(h + 1, 1 - par, 3, h)
                        attend(h, par, 0, 1)
                        if not first:
                            project_out(h - 1, 1 - par, 1, 0, h)
                    if s == 7 and not first:
                        project_out(h - 1, 1 - par, 1, 1, h)
                    if first and (h, s) in FFN_AT:
                        ffn(FFN_AT.index((h, s)))
                    transpose_probs(h, s)

            over_heads(pe, head)
            attend(H - 1, 1, 1, 0)
            attend(H - 1, 1, 1, 1)
            sum_squares(H - 1, 0, H)
            project_out(H - 1, 1, 0, 0, H)
            project_out(H - 1, 1, 0, 1, H)
            sum_squares(H - 1, 1, H)
            project_out(H - 1, 1, 1, 0, H)
            project_out(H - 1, 1, 1, 1, H)

        @block.scalar
        def _(act):
            def copy_qkv(h, k):
                n, pair = NT * h + k, NPAIR * h + k // 2
                act.wait_ge(qkv_ready, n + 1)
                if k % 2 == 0:
                    past(act, v_split, pair - 1)
                    past(act, qk_normed, pair - 1)
                act.activation(stage[:, (k // 2) % 2, k % 2, :], qkv_bank(h, k)[:, 0:3 * D], ACT.Copy).then_inc(qkv_read, 1)

            def square_qk(h, k):
                n = NPAIR * h + k
                act.wait_ge(qkv_read, 2 * n + 2)
                past(act, qk_meansq, n)
                act.activation(squares[:, :, :], stage[:, k % 2, :, 0:2 * D], ACT.Square).then_inc(qk_squared, 1)

            def qk_hi(h, par, k):
                ps = first_ps(k) if isinstance(h, int) and h == 0 else job_ps(f"qkT{k}")
                act.wait_ge(qkT_ready, NPAIR * h + k + 1)
                at = slice(2 * k * P, (2 * k + 2) * P)
                act.activation(qT_hi[:, par, at], ps[:, 0:2 * P], ACT.Copy, scale=q_col[:, 2:3])
                act.activation(kT_hi[:, par, at], ps[:, 2 * P:4 * P], ACT.Copy).then_inc(qkT_hi_done, 1)

            def exps(h, par, s):
                i, n = ORDER[s], NT * h + s
                g, r = RANK[i]
                act.wait_ge(scores_masked, n + 1)
                act.activation(probs[:, s % 2, 0:(i + 1) * P], probs[:, s % 2, 0:(i + 1) * P], ACT.Exp,
                               bias=neg_max[:, par, s:s + 1], scale=-1.0,
                               accum_out=row_sum[:, par, g, r:r + 1]).then_inc(probs_ready, 1)

            def probs_hi(h, s):
                g, r = RANK[ORDER[s]]
                for k, (a, b) in enumerate(CHUNKS[s]):
                    act.wait_ge(pT_ready, CPH * h + CHUNK0[s] + k + 1)
                    act.activation(pT_hi[g][:, a:b, r * P:(r + 1) * P],
                                   pT_ps[(CHUNK0[s] + k) % 2][:, 0:(b - a) * P].rearrange("p (j t) -> p j t", t=P),
                                   ACT.Copy).then_inc(pT_hi_done, 1)

            def y_out(h, g):
                act.wait_ge(yT_ready, 2 * h + g + 1)
                if isinstance(h, int) and (h, g) == (0, 1):
                    act.wait_ge(xq_ready, 2 * NPAIR)
                act.activation(yT_hi[:, g, :], yT_ps[:, :], ACT.Copy).then_inc(y_hi_done, 1)
                act.activation(y_sq[:, g, :], yT_ps[:, :], ACT.Square).then_inc(y_squared, 1)

            def make_bias(h, par):
                past(act, scores_masked, NT * (h - 1))
                act.activation(bias[:, par, :], dist[:, :], ACT.Copy, scale=slopes[:, bass.ds(h, 1)]
                               ).then_inc(bias_ready, 1)

            act.dma_start(w8[:, :, :], ffn_w.rearrange("(k p) i -> p k i", p=P)).then_inc(w8_loaded, 16)
            act.dma_start(q_col[:, 0:1], q_w).then_inc(small_loaded, 16)
            act.dma_start(q_col[:, 1:2], k_w).then_inc(small_loaded, 16)
            act.dma_start(q_col[:, 3:4], sub_w).then_inc(small_loaded, 16)
            act.dma_start(xs_b[:, :], ffn_xs.broadcast_to([P, 1])).then_inc(small_loaded, 16)
            act.dma_start(ffn_s[:, 2:3], ffn_ws.broadcast_to([P, 1])).then_inc(small_loaded, 16)
            act.wait_ge(w_loaded[0], 48)
            act.activation(w_hi[:, 0], w_raw[:, 0], ACT.Copy).then_inc(w_hi_done, 1)
            for n in range(2 * KT):
                half, kt = n // KT, n % KT
                act.wait_ge(xT_ready, n + 1)
                act.activation(xT_hi[:, kt, half * 512:(half + 1) * 512], pT_ps[n % 2][:, :],
                               ACT.Copy).then_inc(xT_hi_done, 1)
            for k in range(NT):
                copy_qkv(0, k)
                if k % 2:
                    square_qk(0, k // 2)
                if k == 3:
                    act.wait_ge(w8T_ready, 1)
                    act.activation(w8T[:, :, :].rearrange("p k o -> p (k o)"), w8T_ps[:, 0:KT * C],
                                   ACT.Copy).then_inc(w8T_read, 1)
            act.wait_ge(const_ready, 3)
            act.wait_ge(wq_col_ready, 1)
            for k in range(NPAIR):
                qk_hi(0, 0, k)
                if k == 1:
                    make_bias(0, 0)

            def head(h, par):
                first, last = isinstance(h, int) and h == 0, is_last(h)
                for s in range(NT):
                    if s % 2:
                        exps(h, par, s)
                    if s > 0:
                        probs_hi(h, s - 1)
                    elif not first:
                        probs_hi(h - 1, NT - 1)
                    if s == 4 and not last:
                        qk_hi(h + 1, 1 - par, 0)
                    if s in (1, 2, 3, 4) and not last:
                        copy_qkv(h + 1, [0, 1, 2, 4, 6][s])
                    if s == 6 and not last:
                        qk_hi(h + 1, 1 - par, 2)
                    if s % 2 == 0:
                        exps(h, par, s)
                    if s == 5 and not last:
                        qk_hi(h + 1, 1 - par, 1)
                    if s == 0 and not last:
                        copy_qkv(h + 1, 0)
                    if s == 1 and not last:
                        square_qk(h + 1, 0)
                    if s == 5 and not last:
                        make_bias(h + 1, 1 - par)
                    if s == 2 and not first:
                        y_out(h - 1, 1)
                    if s in (2, 3, 4) and not last:
                        copy_qkv(h + 1, 2 * s - 1)
                        square_qk(h + 1, s - 1)
                    if s == 6 and not last:
                        qk_hi(h + 1, 1 - par, 3)
                    if s == 7:
                        y_out(h, 0)

            over_heads(act, head)
            probs_hi(H - 1, NT - 1)
            y_out(H - 1, 1)

        @block.vector
        def _(dve):
            steps = [0]

            def link(ins):
                steps[0] += 1
                ins.then_inc(dve_step, 1)
                dve.wait_ge(dve_step, steps[0])

            def mean_squares(h, k):
                n = NPAIR * h + k
                dve.wait_ge(qk_squared, n + 1)
                past(dve, qk_normed, n - 1)
                dve.tensor_reduce(qk_ms[:, k % 2, :], squares[:, :, :].rearrange("p t (a d) -> p (t a) d", d=D),
                                  AX.X, ALU.add).then_inc(qk_summed, 1)
                dve.wait_ge(qk_summed, n + 1)
                dve.tensor_scalar(qk_ms[:, k % 2, :], qk_ms[:, k % 2, :], 1.0 / D, EPS,
                                  ALU.mult, ALU.add).then_inc(qk_meansq, 1)

            def split_v(h, par, k):
                n = NPAIR * h + k
                dve.wait_ge(qkv_read, 2 * n + 2)
                past(dve, yT_ready, 2 * (h - 1))
                v = stage[:, k % 2, :, 2 * D:3 * D]
                dve.tensor_copy(v_hi[:, par, 2 * k:2 * k + 2, :], v).then_inc(v_hi_done, 1)
                dve.wait_ge(v_hi_done, n + 1)
                dve.tensor_tensor(v_lo[:, par, 2 * k:2 * k + 2, :], v, v_hi[:, par, 2 * k:2 * k + 2, :].bitcast(f32),
                                  ALU.subtract).then_inc(v_split, 1)

            def qk_lo(h, par, k):
                ps = first_ps(k) if isinstance(h, int) and h == 0 else job_ps(f"qkT{k}")
                dve.wait_ge(qkT_hi_done, NPAIR * h + k + 1)
                at = slice(2 * k * P, (2 * k + 2) * P)
                dve.scalar_tensor_tensor(qT_lo[:, par, at], ps[:, 0:2 * P], q_col[:, 2:3],
                                         qT_hi[:, par, at].bitcast(f32), ALU.mult, ALU.subtract)
                dve.tensor_tensor(kT_lo[:, par, at], ps[:, 2 * P:4 * P], kT_hi[:, par, at].bitcast(f32),
                                  ALU.subtract).then_inc(misc_read, 1)

            def mask(h, par, s):
                i, n = ORDER[s], NT * h + s
                ps, at, _ = score_at(i)
                w = (i + 1) * P
                dve.wait_ge(scores_ready, n + 1)
                if s == 0:
                    dve.wait_ge(bias_ready, h + 1)
                s2, h2 = (s - 2, h) if s >= 2 else (s - 2 + NT, h - 1)
                past(dve, pT_ready, CPH * h2 + CHUNK0[s2 + 1])
                dve.nop(nofuse=True)
                dve.tensor_tensor_reduce(out=probs[:, s % 2, 0:w], in0=ps[:, at:at + w],
                                         in1=bias[:, par, (NT - 1 - i) * P:(NT - 1 - i) * P + w],
                                         scale=1.0, scalar=3.0e38, op0=ALU.add, op1=ALU.min,
                                         accum_out=neg_max[:, par, s:s + 1]).then_inc(scores_masked, 1)

            def probs_lo(h, s):
                g, r = RANK[ORDER[s]]
                for k, (a, b) in enumerate(CHUNKS[s]):
                    dve.wait_ge(pT_hi_done, CPH * h + CHUNK0[s] + k + 1)
                    dve.tensor_tensor(pT_lo[g][:, a:b, r * P:(r + 1) * P],
                                      pT_ps[(CHUNK0[s] + k) % 2][:, 0:(b - a) * P].rearrange("p (j t) -> p j t", t=P),
                                      pT_hi[g][:, a:b, r * P:(r + 1) * P].bitcast(f32),
                                      ALU.subtract).then_inc(pT_split, 1)

            def y_lo(h, g):
                dve.wait_ge(y_squared, 2 * h + g + 1)
                dve.tensor_tensor(yT_lo[:, g, :], yT_ps[:, :], yT_hi[:, g, :].bitcast(f32),
                                  ALU.subtract).then_inc(y_split, 1)

            def y_mean(h, par, g):
                dve.scalar_tensor_tensor(y_el2[:, g, :], row_sum[:, par, g, :], EPS, row_sum[:, par, g, :],
                                         ALU.mult, ALU.mult).then_inc(el2_ready, 1)
                dve.wait_ge(el2_ready, 2 * h + g + 1)
                dve.wait_ge(ss_ready, 2 * h + g + 1)
                dve.scalar_tensor_tensor(y_ms[:, g, :], job_ps(f"ss{g}")[:, 0:4], 1.0 / D, y_el2[:, g, :],
                                         ALU.mult, ALU.add).then_inc(misc_read, 1)

            def add_out(h, g, half):
                dve.wait_ge(proj_ready, 4 * h + 2 * g + half + 1)
                dve.wait_ge(y_normed, 2 * h + g + 1)
                for r in (2 * half, 2 * half + 1):
                    t = GROUPS[g][r]
                    last = dve.scalar_tensor_tensor(acc[:, t, :], job_ps(f"proj{g}{'ab'[half]}")[:, (r % 2) * C:(r % 2 + 1) * C],
                                                    y_r[:, g, r:r + 1], acc[:, t, :], ALU.mult, ALU.add)
                last.then_inc(misc_read, 1)

            for n in range(2):
                tiles = range(n * NT // 2, (n + 1) * NT // 2)
                at = slice(tiles[0], tiles[-1] + 1)
                dve.wait_ge(x_loaded[n], 16 * NPAIR // 2)
                for t in tiles:
                    last = dve.bn_stats(stats[:, t, :], acc[:, t, :])
                link(last)
                for t in tiles:
                    last = dve.bn_aggr(mean_var[:, t, :], stats[:, t, :])
                link(last)
                dve.tensor_scalar(rstd[:, at], mean_var[:, at, 1], EPS, None, ALU.add).then_inc(var_ready, 1)

            for n in range(2):
                dve.wait_ge(rstd_ready, n + 1)
                for t in range(n * NT // 2, (n + 1) * NT // 2):
                    dve.tensor_scalar(bias_xn(t), acc[:, t, :], mean_var[:, t, 0:1], rstd[:, t:t + 1],
                                      ALU.subtract, ALU.mult).then_inc(xn_ready, 1)
            dve.wait_ge(w_hi_done, 1)
            dve.tensor_tensor(w_lo[:, 0], w_raw[:, 0], w_hi[:, 0].bitcast(f32), ALU.subtract).then_inc(w_split, 1)
            dve.wait_ge(small_loaded, 80)
            dve.scalar_tensor_tensor(q_col[:, 2:3], q_col[:, 0:1], -SCALE, q_col[:, 1:2],
                                     ALU.mult, ALU.mult).then_inc(wq_col_ready, 1)
            for n in range(2 * KT):
                half, kt = n // KT, n % KT
                at = slice(half * 512, (half + 1) * 512)
                dve.wait_ge(xT_hi_done, n + 1)
                dve.tensor_tensor(xT_lo[:, kt, at], pT_ps[n % 2][:, :], xT_hi[:, kt, at].bitcast(f32),
                                  ALU.subtract).then_inc(xT_read, 1)

            def quantize_x(n):
                pair, kt = n // KT, n % KT
                at = slice(pair * 2 * P, (pair + 1) * 2 * P)
                u, m = y_sq[:, 1, 0:2 * P], y_sq[:, 1, 2 * P:4 * P]
                link(dve.tensor_tensor(u, xT_hi[:, kt, at].bitcast(f32), xT_lo[:, kt, at].bitcast(f32), ALU.add))
                link(dve.tensor_scalar(u, u, ffn_s[:, 1:2], E4M3_MAX, ALU.mult, ALU.min))
                link(dve.tensor_scalar(u, u, -E4M3_MAX, None, ALU.max))
                link(dve.tensor_scalar(m.bitcast(i32), u.bitcast(i32), 0x7F800000, None, ALU.bitwise_and))
                link(dve.tensor_scalar(m, m, 2.0 ** -6, 1.5 * 2.0 ** 20, ALU.max, ALU.mult))
                link(dve.tensor_tensor(u, u, m, ALU.add))
                dve.tensor_tensor(xqT[:, kt, at], u, m, ALU.subtract).then_inc(xq_ready, 1)
                dve.wait_ge(xq_ready, n + 1)

            u = probs[:, :, :].rearrange("p a t -> p (a t)")
            dve.wait_ge(w8_loaded, 16)
            code = u[:, 0:KT * C].bitcast(i32)
            mag = u[:, KT * C:2 * KT * C]
            alt = u[:, 2 * KT * C:3 * KT * C]
            sign = u[:, 3 * KT * C:4 * KT * C]
            link(dve.tensor_copy(code, w8[:, :, :].rearrange("p k i -> p (k i)")))
            dve.tensor_scalar(sign, code, 128, -2.0, ALU.is_ge, ALU.mult)
            link(dve.tensor_scalar(mag.bitcast(i32), code, 0x7F, 20, ALU.bitwise_and, ALU.logical_shift_left))
            link(dve.tensor_scalar(mag.bitcast(i32), mag.bitcast(i32), 112 << 23, None, ALU.bitwise_or))
            link(dve.tensor_scalar(mag, mag, 256.0, None, ALU.mult))
            link(dve.tensor_scalar(alt, mag, 2.0, -(2.0 ** -6), ALU.mult, ALU.add))
            link(dve.tensor_tensor(mag, mag, alt, ALU.min))
            dve.scalar_tensor_tensor(wb[:, :, :].rearrange("p k i -> p (k i)"), sign, 1.0, mag,
                                     ALU.add, ALU.mult).then_inc(wb_ready, 1)
            link(dve.tensor_copy(ffn_s[:, 0:1], xs_b[:, :]))
            link(dve.reciprocal(ffn_s[:, 1:2], ffn_s[:, 0:1]))
            dve.tensor_tensor(ffn_s[:, 3:4], ffn_s[:, 0:1], ffn_s[:, 2:3], ALU.mult)
            for k in range(NPAIR):
                mean_squares(0, k)
                split_v(0, 0, k)
                if (-1, k) in QUANTIZE_AT:
                    quantize_x(QUANTIZE_AT.index((-1, k)))
                if k >= 2:
                    qk_lo(0, 0, k - 2)
            qk_lo(0, 0, 2)
            qk_lo(0, 0, 3)
            mask(0, 0, 0)

            def add_ffn(n):
                dve.wait_ge(ffn_ready, n + 1)
                for t in (2 * n, 2 * n + 1):
                    last = dve.scalar_tensor_tensor(acc[:, t, :], yT_ps[:, (t % 2) * C:(t % 2 + 1) * C],
                                                    ffn_s[:, 3:4], acc[:, t, :], ALU.mult, ALU.add)
                last.then_inc(ffn_added, 1)

            def head(h, par):
                first, last = isinstance(h, int) and h == 0, is_last(h)
                for s in range(NT):
                    if s in (3, 5) and not last:
                        mean_squares(h + 1, 1 if s == 3 else 3)
                    if s > 0:
                        probs_lo(h, s - 1)
                    elif not first:
                        probs_lo(h - 1, NT - 1)
                    if s in (4, 5) and not last:
                        qk_lo(h + 1, 1 - par, s - 4)
                    if s == 6 and not last:
                        qk_lo(h + 1, 1 - par, 2)
                    if s < NT - 1:
                        mask(h, par, s + 1)
                    elif not last:
                        mask(h + 1, 1 - par, 0)
                    if isinstance(h, int) and (h, s) in QUANTIZE_AT:
                        quantize_x(QUANTIZE_AT.index((h, s)))
                    if s == 0 and not first:
                        if not (isinstance(h, int) and h == 1):
                            add_out(h - 2, 1, 1)
                        y_mean(h - 1, 1 - par, 0)
                    if s == 6 and not last:
                        qk_lo(h + 1, 1 - par, 3)
                    if s == 1 and not last:
                        mean_squares(h + 1, 0)
                    if isinstance(h, int) and h > 0 and (h, s) in FFN_AT:
                        add_ffn(FFN_AT.index((h, s)))
                    if s == 4 and not first:
                        y_mean(h - 1, 1 - par, 1)
                    if s in (2, 3, 4, 5) and not last:
                        split_v(h + 1, 1 - par, s - 2)
                    if first and (h, s) in FFN_AT:
                        add_ffn(FFN_AT.index((h, s)))
                    if s in (2, 3) and not first:
                        add_out(h - 1, 0, s - 2)
                    if s == 3 and not last:
                        mean_squares(h + 1, 2)
                    if s == 2 and not first:
                        y_lo(h - 1, 1)
                    if s == 6 and not first:
                        add_out(h - 1, 1, 0)
                    if s == 7:
                        y_lo(h, 0)

            over_heads(dve, head)
            probs_lo(H - 1, NT - 1)
            add_out(H - 2, 1, 1)
            y_mean(H - 1, 1, 0)
            y_lo(H - 1, 1)
            add_out(H - 1, 0, 0)
            add_out(H - 1, 0, 1)
            y_mean(H - 1, 1, 1)
            add_out(H - 1, 1, 0)
            add_out(H - 1, 1, 1)


def kernel(L0_attn_x, L0_attn_Wq, L0_attn_Wk, L0_attn_Wv, L0_attn_Wproj, L0_attn_q_rms_w, L0_attn_k_rms_w,
           L0_attn_subln_w, L0_ffn_weight, L0_ffn_weight_scale, L0_ffn_input_scale):
    import concourse.bacc as bacc
    from concourse.bass_utils import run_bass_kernel_spmd

    nc = bacc.Bacc("TRN2", target_bir_lowering=False, num_devices=1)
    shaped = {
        "x": np.asarray(L0_attn_x)[0],
        "wq": L0_attn_Wq, "wk": L0_attn_Wk, "wv": L0_attn_Wv, "wproj": L0_attn_Wproj,
        "q_w": np.asarray(L0_attn_q_rms_w).reshape(-1, 1),
        "k_w": np.asarray(L0_attn_k_rms_w).reshape(-1, 1),
        "sub_w": np.asarray(L0_attn_subln_w).reshape(-1, 1),
        "ffn_w": np.asarray(L0_ffn_weight).view(np.uint8),
        "ffn_ws": np.asarray(L0_ffn_weight_scale).reshape(1, 1),
        "ffn_xs": np.asarray(L0_ffn_input_scale).reshape(1, 1),
    }
    arrays, aps = {}, {}
    for name, a in shaped.items():
        a = np.ascontiguousarray(a)
        arrays["in_" + name] = a
        aps[name] = nc.dram_tensor("in_" + name, a.shape, mybir.dt.from_np(a.dtype), kind="ExternalInput").ap()
    rows, cols = shaped["x"].shape
    out = nc.dram_tensor("out", (rows, cols), mybir.dt.float32, kind="ExternalOutput").ap()
    build_block(nc, out=out, **aps)
    got = run_bass_kernel_spmd(nc, [arrays], core_ids=[0])
    return got.results[0]["out"].reshape(1, rows, cols)
```

```python
import numpy as np
import concourse.bass as bass
from concourse import mybir
from contextlib import ExitStack



def build_block(nc, x, wq, wk, wv, wproj, q_w, k_w, sub_w, ffn_w, ffn_ws, ffn_xs, out):
    f32, f32r, bf16 = mybir.dt.float32, mybir.dt.float32r, mybir.dt.bfloat16
    i32, u8 = mybir.dt.int32, mybir.dt.uint8
    ALU, ACT, AX = mybir.AluOpType, mybir.ActivationFunctionType, mybir.AxisListType

    P = 128
    T, C = x.shape[0], x.shape[1]
    D = q_w.shape[0]
    H = wq.shape[1] // D
    NT = T // P
    KT = C // P
    NPAIR = NT // 2
    EPS = 1e-5
    SCALE = float(D) ** -0.5
    BIG = 1e30
    E4M3_MAX = 448.0

    ORDER = [7, 0, 6, 1, 5, 2, 4, 3]
    GROUPS = [sorted(ORDER[:4], reverse=True), sorted(ORDER[4:], reverse=True)]
    RANK = {i: (g, GROUPS[g].index(i)) for g in range(2) for i in GROUPS[g]}
    CHUNKS = [[(j, min(j + 4, i + 1)) for j in range(0, i + 1, 4)] for i in ORDER]
    CHUNK0 = [sum(len(c) for c in CHUNKS[:s]) for s in range(NT + 1)]
    CPH = CHUNK0[NT]

    MISC = ["ss0", "proj0a", "proj0b", "qkT0", "ss1", "qkT1", "qkT2", "qkT3", "proj1a", "proj1b"]
    JOB_BANK = {"ss0": "qkv", "proj0b": "yT", "ss1": "yT", "qkT2": "qkv", "proj1a": "qkv"}
    TAIL_BANK = {"ss0": "qkv", "proj0a": "small", "proj0b": None, "ss1": "big0", "proj1a": "qkv", "proj1b": "big1"}
    MISC_FIRST = [m for m in MISC if m.startswith("qkT")]
    MISC_LAST = [m for m in MISC if not m.startswith("qkT")]
    MISC_TAIL = ["ss0", "proj0a", "proj0b", "ss1", "proj1a", "proj1b"]

    def misc_done(h, job):
        if isinstance(h, int) and h < 0:
            return int(job[3]) + 1
        if isinstance(h, int) and h == 0:
            return NPAIR + MISC_FIRST.index(job) + 1
        base = NPAIR + len(MISC_FIRST) + (h - 1) * len(MISC)
        if isinstance(h, int) and h == H - 1:
            return base + MISC_LAST.index(job) + 1
        if isinstance(h, int) and h == H:
            return base - len(MISC) + len(MISC_LAST) + MISC_TAIL.index(job) + 1
        return base + MISC.index(job) + 1

    def past(eng, sem, count):
        if not isinstance(count, int) or count > 0:
            eng.wait_ge(sem, count)

    ctx = ExitStack()
    with ctx:
        def sb(name, shape, dt=f32):
            return ctx.enter_context(nc.sbuf_tensor(name, shape, dt))

        def pb(name, shape, dt=f32):
            return ctx.enter_context(nc.psum_tensor(name, shape, dt))

        def sem(name):
            return ctx.enter_context(nc.semaphore(name))

        ident = sb("ident", [P, P])
        ident_b = sb("ident_b", [P, P], bf16)
        ones = sb("ones", [P, 1])
        minus_half = sb("minus_half", [P, NT])
        slopes = sb("slopes", [P, H])
        dist = sb("dist", [P, T])
        acc = sb("acc", [P, NT, C])
        xT_hi = sb("xT_hi", [P, KT, T], f32r)
        xT_lo = sb("xT_lo", [P, KT, T], f32r)
        w_raw = sb("w_raw", [P, 2, KT, 3 * D])
        w_hi = sb("w_hi", [P, 2, KT, 3 * D], f32r)
        w_lo = sb("w_lo", [P, 2, KT, 3 * D], f32r)
        wp_raw = sb("wp_raw", [P, 2, C])
        wp_hi = sb("wp_hi", [P, 2, C], f32r)
        wp_lo = sb("wp_lo", [P, 2, C], f32r)
        stage = sb("stage", [P, 2, 2, 3 * D])
        squares = sb("squares", [P, 2, 2 * D])
        qk_ms = sb("qk_ms", [P, 2, 4])
        qk_r = sb("qk_r", [P, 2, 4])
        qk_n = sb("qk_n", [P, 2, 2, 2, D])
        qT_hi = sb("qT_hi", [P, 2, T], f32r)
        qT_lo = sb("qT_lo", [P, 2, T], f32r)
        kT_hi = sb("kT_hi", [P, 2, T], f32r)
        kT_lo = sb("kT_lo", [P, 2, T], f32r)
        v_hi = sb("v_hi", [P, 2, NT, D], f32r)
        v_lo = sb("v_lo", [P, 2, NT, D], f32r)
        bias = sb("bias", [P, 2, T])
        probs = sb("probs", [P, 2, T])
        neg_max = sb("neg_max", [P, 2, NT])
        row_sum = sb("row_sum", [P, 2, 2, 4])
        pT_hi = [sb(f"pT_hi{g}", [P, GROUPS[g][0] + 1, 4 * P], f32r) for g in range(2)]
        pT_lo = [sb(f"pT_lo{g}", [P, GROUPS[g][0] + 1, 4 * P], f32r) for g in range(2)]
        yT_hi = sb("yT_hi", [P, 2, 4 * P], f32r)
        yT_lo = sb("yT_lo", [P, 2, 4 * P], f32r)
        y_sq = sb("y_sq", [P, 2, 4 * P])
        y_ms = sb("y_ms", [P, 2, 4])
        y_el2 = sb("y_el2", [P, 2, 4])
        y_r = sb("y_r", [P, 2, 4])
        q_col = sb("q_col", [P, 4])
        stats = sb("stats", [P, NT, 6])
        mean_var = sb("mean_var", [P, NT, 2])
        rstd = sb("rstd", [P, NT])
        xs_b = sb("xs_b", [P, 1], bf16)
        ffn_s = sb("ffn_s", [P, 4])
        w8 = sb("w8", [P, KT, C], mybir.dt.from_np(np.dtype("uint8")))
        wb = sb("wb", [P, KT, C], bf16)
        w8T = sb("w8T", [P, KT, C], bf16)
        xqT = sb("xqT", [P, KT, P], bf16)

        score_big = pb("score_big", [P, 1024])
        score_small = pb("score_small", [P, 512])
        pT_ps = [pb(f"pT_ps{b}", [P, 512]) for b in range(2)]
        yT_ps = pb("yT_ps", [P, 512])
        qkv_ps = pb("qkv_ps", [P, 512])
        misc = pb("misc", [P, 512])

        x_loaded = [sem(f"x_loaded{n}") for n in range(2)]
        small_loaded = sem("small_loaded")
        w8_loaded = sem("w8_loaded")
        w_loaded = [sem(f"w_loaded{b}") for b in range(2)]
        wp_loaded = [sem(f"wp_loaded{b}") for b in range(2)]
        w_split = sem("w_split")
        wp_split = sem("wp_split")
        const_ready = sem("const_ready")
        pool_step = sem("pool_step")
        dve_step = sem("dve_step")
        xn_ready = sem("xn_ready")
        xT_ready = sem("xT_ready")
        xT_hi_done = sem("xT_hi_done")
        xT_read = sem("xT_read")
        var_ready = sem("var_ready")
        rstd_ready = sem("rstd_ready")
        wb_ready = sem("wb_ready")
        w8T_ready = sem("w8T_ready")
        w8T_read = sem("w8T_read")
        x_stepped = sem("x_stepped")
        xq_ready = sem("xq_ready")
        ffn_ready = sem("ffn_ready")
        ffn_added = sem("ffn_added")
        qkv_ready = sem("qkv_ready")
        qkv_read = sem("qkv_read")
        qk_squared = sem("qk_squared")
        qk_meansq = sem("qk_meansq")
        qk_normed = sem("qk_normed")
        qk_summed = sem("qk_summed")
        qk_r_ready = sem("qk_r_ready")
        w_hi_done = sem("w_hi_done")
        wp_scaled = sem("wp_scaled")
        wp_hi_done = sem("wp_hi_done")
        wq_col_ready = sem("wq_col_ready")
        qkT_ready = sem("qkT_ready")
        qkT_hi_done = sem("qkT_hi_done")
        v_hi_done = sem("v_hi_done")
        v_split = sem("v_split")
        bias_ready = sem("bias_ready")
        scores_ready = sem("scores_ready")
        scores_masked = sem("scores_masked")
        probs_ready = sem("probs_ready")
        pT_ready = sem("pT_ready")
        pT_hi_done = sem("pT_hi_done")
        pT_split = sem("pT_split")
        yT_ready = sem("yT_ready")
        y_hi_done = sem("y_hi_done")
        y_squared = sem("y_squared")
        y_split = sem("y_split")
        ss_ready = sem("ss_ready")
        el2_ready = sem("el2_ready")
        y_normed = sem("y_normed")
        proj_ready = sem("proj_ready")
        misc_read = sem("misc_read")
        stored = sem("stored")

        block = ctx.enter_context(nc.Block())

        wq_v = wq.rearrange("(k p) (h d) -> p k h d", p=P, d=D)
        wk_v = wk.rearrange("(k p) (h d) -> p k h d", p=P, d=D)
        wv_v = wv.rearrange("(k p) (h d) -> p k h d", p=P, d=D)
        wp_v = wproj.rearrange("(h p) c -> p h c", p=P)
        x_v = x.rearrange("(t p) c -> p t c", p=P)
        out_v = out.rearrange("(t p) c -> p t c", p=P)

        def over_heads(eng, body):
            body(0, 0, None)
            body(1, 1, 0)
            with eng.Fori(1, H // 2 - 1) as pair:
                body(pair * 2, 0, pair)
                body(pair * 2 + 1, 1, None)
            body(H - 2, 0, NT - 1)
            body(H - 1, 1, None)

        def scale_qk(eng, h, k):
            eng.tensor_tensor(
                qk_n[:, k % 2], stage_of(h, k)[:, :, 0:2 * D].rearrange("p t (a d) -> p t a d", d=D),
                qk_r[:, k % 2, :].rearrange("p (t a) -> p t a", a=2).unsqueeze(3).broadcast_to([P, 2, 2, D]),
                ALU.mult).then_inc(qk_normed, 1)

        w8T_ps = pT_ps[0][:, :].bitcast(bf16)

        def qkv_bank(h, k):
            return yT_ps if isinstance(h, int) and k % 2 and (h == 0 or h == 1 and k <= 5) else qkv_ps

        def xT_bank(n):
            return (pT_ps[0][:, :], pT_ps[1][:, :], misc[:, :], score_small[:, :])[n]

        def first_ps(k):
            return (misc[:, :], score_small[:, :], score_big[:, 0:4 * P], score_big[:, 4 * P:8 * P])[k]

        def stage_of(h, k):
            if isinstance(h, int) and h == 0 and k >= 2:
                room = bias[:, 1, :] if k == 2 else probs[:, 1, :]
                return room[:, 0:6 * D].rearrange("p (t n) -> p t n", t=2)
            return stage[:, k % 2]

        def squares_of(h, k):
            if isinstance(h, int) and h == 0 and k % 2:
                return y_sq[:, 0, :].rearrange("p (t n) -> p t n", t=2)
            return squares[:, :, :]

        def bank_of(h, job):
            if isinstance(h, int) and h == H:
                return TAIL_BANK[job]
            if is_last(h) and job == "ss1":
                return None
            return JOB_BANK.get(job)

        def job_ps(h, job):
            return {"yT": yT_ps[:, :], "qkv": qkv_ps[:, :], "small": score_small[:, :], "big0": score_big[:, 0:4 * P],
                    "big1": score_big[:, 4 * P:8 * P]}.get(bank_of(h, job), misc[:, :])

        def bias_xn(t):
            return bias[:, t // 4, (t % 4) * C:(t % 4 + 1) * C]

        def is_last(h):
            return isinstance(h, int) and h == H - 1

        def score_at(i):
            w = (i + 1) * P
            if i < 4:
                return score_small, 0, [(0, w)]
            if w == 640:
                return score_big, 128, [(0, 384), (384, 640)]
            return score_big, 0, [(0, 512), (512, w)]

        @block.sync
        def _(sp):
            for n in range(2):
                half = slice(n * NT // 2, (n + 1) * NT // 2)
                sp.dma_start(acc[:, half, :], x_v[:, half, :]).then_inc(x_loaded[n], 16)

            def load_w(h, par):
                for n, w in enumerate((wq_v, wk_v, wv_v)):
                    sp.dma_start(w_raw[:, par, :, n * D:(n + 1) * D], w[:, :, h, :]).then_inc(w_loaded[par], 16)

            def load_wp(h, par):
                sp.dma_start(wp_raw[:, par, :], wp_v[:, h, :]).then_inc(wp_loaded[par], 16)

            load_w(0, 0)
            load_w(1, 1)
            load_wp(0, 0)

            def head(h, par, tile):
                if not (isinstance(h, int) and h + 2 >= H):
                    sp.wait_ge(w_split, h + 1)
                    load_w(h + 2, par)
                if not is_last(h):
                    past(sp, wp_split, h)
                    load_wp(h + 1, 1 - par)

            over_heads(sp, head)
            for g in range(2):
                for n, i in enumerate(GROUPS[g]):
                    if n % 2 == 0:
                        sp.wait_ge(misc_read, misc_done(H, f"proj{g}{'ab'[n // 2]}"))
                    sp.dma_start(out_v[:, i, :], acc[:, i, :]).then_inc(stored, 16)
            sp.wait_ge(stored, 16 * NT)

        @block.gpsimd
        def _(pool):
            steps = [0]

            def link(ins):
                steps[0] += 1
                ins.then_inc(pool_step, 1)
                pool.wait_ge(pool_step, steps[0])

            pool.memset(minus_half[:, :], -0.5)
            link(pool.memset(ident[:, :], 0.0))
            pool.affine_select(out=ident[:, :], in_=ident[:, :], compare_op=ALU.not_equal, fill=1.0, base=0,
                               pattern=[[-1, P]], channel_multiplier=1).then_inc(const_ready, 1)
            pool.wait_ge(const_ready, 1)
            pool.tensor_copy(ident_b[:, :], ident[:, :]).then_inc(const_ready, 1)
            pool.memset(ones[:, :], 1.0)
            for h in range(H):
                pool.memset(slopes[:, h:h + 1], float(np.float32(2.0 ** (-0.5 * (h + 1)))))
            for n in range(2):
                at = slice(n * NT // 2, (n + 1) * NT // 2)
                pool.wait_ge(var_ready, n + 1)
                pool.tensor_tensor(rstd[:, at], rstd[:, at], minus_half[:, at], ALU.pow).then_inc(rstd_ready, 1)

            link(pool.iota(dist[:, :], pattern=[[-1, T]], base=T - P, channel_multiplier=1,
                           allow_small_or_imprecise_dtypes=True))
            pool.affine_select(out=dist[:, :], in_=dist[:, :], compare_op=ALU.is_ge, fill=BIG, base=T - P,
                               pattern=[[-1, T]], channel_multiplier=1).then_inc(const_ready, 1)

            def split_w(h, par):
                pool.wait_ge(w_loaded[par], 48 * (h // 2 + 1) if isinstance(h, int) else (h - par) * 24 + 48)
                past(pool, qkv_ready, (h - 1) * NT)
                pool.nop(nofuse=True)
                pool.tensor_copy(w_hi[:, par], w_raw[:, par]).then_inc(w_hi_done, 1)
                pool.wait_ge(w_hi_done, h + 1)
                pool.tensor_tensor(w_lo[:, par], w_raw[:, par], w_hi[:, par].bitcast(f32),
                                   ALU.subtract).then_inc(w_split, 1)

            def split_wp(h, par):
                pool.wait_ge(wp_loaded[par], 16 * (h // 2 + 1) if isinstance(h, int) else (h - par) * 8 + 16)
                past(pool, proj_ready, (h - 1) * 4)
                pool.nop(nofuse=True)
                pool.tensor_scalar(wp_raw[:, par], wp_raw[:, par], q_col[:, 3:4], None,
                                   ALU.mult).then_inc(wp_scaled, 1)
                pool.wait_ge(wp_scaled, h + 1)
                pool.nop(nofuse=True)
                pool.tensor_copy(wp_hi[:, par], wp_raw[:, par]).then_inc(wp_hi_done, 1)
                pool.wait_ge(wp_hi_done, h + 1)
                pool.tensor_tensor(wp_lo[:, par], wp_raw[:, par], wp_hi[:, par].bitcast(f32),
                                   ALU.subtract).then_inc(wp_split, 1)

            def norm_qk(h, k):
                n = NPAIR * h + k
                pool.wait_ge(qk_meansq, n + 1)
                pool.tensor_tensor(qk_r[:, k % 2, :], qk_ms[:, k % 2, :], minus_half[:, 0:4],
                                   ALU.pow).then_inc(qk_r_ready, 1)
                if isinstance(h, int) and h == 0:
                    return
                pool.wait_ge(qk_r_ready, n + 1)
                past(pool, qkT_ready, n - 1)
                scale_qk(pool, h, k)

            def norm_y(h, g, now):
                pool.wait_ge(misc_read, misc_done(now, f"ss{g}"))
                pool.tensor_tensor(y_r[:, g, :], y_ms[:, g, :], minus_half[:, 0:4], ALU.pow).then_inc(y_normed, 1)

            pool.wait_ge(w_split, 1)
            split_w(1, 1)
            for k in range(NPAIR):
                norm_qk(0, k)
            pool.wait_ge(small_loaded, 80)

            def head(h, par, tile):
                first, last = isinstance(h, int) and h == 0, is_last(h)
                if not first:
                    norm_y(h - 1, 0, h)
                if not (isinstance(h, int) and h + 2 >= H):
                    split_w(h + 2, par)
                if not last:
                    norm_qk(h + 1, 0)
                    norm_qk(h + 1, 1)
                    norm_qk(h + 1, 2)
                if not first:
                    norm_y(h - 1, 1, h)
                if not last:
                    norm_qk(h + 1, 3)
                split_wp(h, par)

            over_heads(pool, head)
            norm_y(H - 1, 0, H)
            norm_y(H - 1, 1, H)

        @block.tensor
        def _(pe):
            def product(dst, a_hi, a_lo, b_hi, b_lo, start=True, stop=True):
                pe.matmul(dst, a_hi, b_hi, start=start, stop=False)
                pe.matmul(dst, a_hi, b_lo, start=False, stop=False)
                return pe.matmul(dst, a_lo, b_hi, start=False, stop=stop)

            def bank_free(h, job):
                if isinstance(h, int) and h < 0:
                    return
                tail = isinstance(h, int) and h == H
                jobs = MISC_TAIL if tail else MISC_LAST if is_last(h) else MISC
                if isinstance(h, int) and h == 0:
                    jobs = MISC_FIRST
                bank = bank_of(h, job)
                if tail and bank in ("small", "big0", "big1"):
                    pe.wait_ge(scores_masked, NT * H)
                    return
                if job == "ss0":
                    pe.wait_ge(qkv_read, min(NT * (h + 1) + 1, NT * H) if isinstance(h, int) else NT * h + NT + 1)
                    pe.wait_ge(misc_read, misc_done(h - 1, "qkT2" if isinstance(h, int) and h == 1 else "proj1a"))
                    return
                same = [m for m in jobs[:jobs.index(job)] if bank_of(h, m) == bank and (m != "ss0" or tail)]
                if same:
                    pe.wait_ge(misc_read, misc_done(h, same[-1]))
                elif bank == "qkv":
                    pe.wait_ge(qkv_read, NT * (min(h + 2, H) if isinstance(h, int) else h + 2))
                elif bank == "yT":
                    pe.wait_ge(y_split, 2 * h)
                else:
                    before = "qkT3" if isinstance(h, int) and h <= 1 else "proj1b"
                    pe.wait_ge(misc_read, misc_done(h - 1, before))

            def project(h, par, k):
                if k == 0:
                    pe.wait_ge(w_split, h + 1)
                past(pe, qkv_read, NT * h + k - (1 if isinstance(h, int) and (h == 0 or h == 1 and 1 <= k <= 6) else 0))
                if k == 0 and not (isinstance(h, int) and h <= 1):
                    pe.wait_ge(misc_read, misc_done(h - 2, "proj1a" if not (isinstance(h, int) and h == 2) else "qkT2"))
                if k == 1 and not (isinstance(h, int) and h <= 1):
                    pe.wait_ge(misc_read, misc_done(h - 1, "ss0"))
                for kt in range(KT):
                    at = (slice(None), kt, slice(k * P, (k + 1) * P))
                    last = product(qkv_bank(h, k)[:, 0:3 * D], xT_hi[at], xT_lo[at], w_hi[:, par, kt], w_lo[:, par, kt],
                                   start=kt == 0, stop=kt == KT - 1)
                last.then_inc(qkv_ready, 1)

            def transpose_qk(h, par, k, now):
                bank_free(now, f"qkT{k}")
                pe.wait_ge(qk_normed, NPAIR * h + k + 1)
                ps = first_ps(k) if isinstance(now, int) and now < 0 else job_ps(0, f"qkT{k}")
                for a in range(2):
                    for t in range(2):
                        last = pe.transpose(ps[:, (2 * a + t) * P:(2 * a + t + 1) * P],
                                            qk_n[:, k % 2, t, a, :], ident[:, :])
                last.then_inc(qkT_ready, 1)

            def score(h, par, s):
                i, n = ORDER[s], NT * h + s
                if s == 0:
                    pe.wait_ge(misc_read, misc_done(h - 1, "qkT3"))
                past(pe, scores_masked, n - 1)
                ps, at, parts = score_at(i)
                q = (slice(None), par, slice(i * P, (i + 1) * P))
                for a, b in parts:
                    last = product(ps[:, at + a:at + b], qT_hi[q], qT_lo[q], kT_hi[:, par, a:b], kT_lo[:, par, a:b])
                last.then_inc(scores_ready, 1)

            def transpose_probs(h, s):
                pe.wait_ge(probs_ready, NT * h + s + 1)
                for k, (a, b) in enumerate(CHUNKS[s]):
                    c = CPH * h + CHUNK0[s] + k
                    ps = pT_ps[(CHUNK0[s] + k) % 2]
                    past(pe, pT_split, c - 1)
                    for j in range(a, b):
                        last = pe.transpose(ps[:, (j - a) * P:(j - a + 1) * P],
                                            probs[:, s % 2, j * P:(j + 1) * P], ident[:, :])
                    last.then_inc(pT_ready, 1)

            def attend(h, par, g, half):
                nj = GROUPS[g][0] + 1
                weight = [sum(i >= j for i in GROUPS[g]) for j in range(nj)]
                cut = next(j for j in range(nj + 1) if 2 * sum(weight[:j]) >= sum(weight))
                if half == 0:
                    pe.wait_ge(pT_split, CPH * h + CHUNK0[4 * (g + 1)])
                    pe.wait_ge(v_split, NPAIR * (h + 1))
                    past(pe, y_split, 2 * h + g)
                    if g == 0 and not (isinstance(h, int) and h == 0):
                        pe.wait_ge(misc_read, misc_done(h, "ss1"))
                    elif g == 0:
                        pe.wait_ge(qkv_read, NT + 6)
                for j in range(0, cut) if half == 0 else range(cut, nj):
                    w = weight[j] * P
                    last = product(yT_ps[:, 0:w], v_hi[:, par, j, :], v_lo[:, par, j, :],
                                   pT_hi[g][:, j, 0:w], pT_lo[g][:, j, 0:w], start=j == 0, stop=j == nj - 1)
                if half == 1:
                    last.then_inc(yT_ready, 1)

            def sum_squares(h, g, now):
                bank_free(now, f"ss{g}")
                pe.wait_ge(y_squared, 2 * h + g + 1)
                for r in range(4):
                    last = pe.matmul(job_ps(h + 1, f"ss{g}")[:, r:r + 1], y_sq[:, g, r * P:(r + 1) * P], ones[:, 0:1],
                                     start=True, stop=True)
                last.then_inc(ss_ready, 1)

            def project_out(h, par, g, half, now):
                bank_free(now, f"proj{g}{'ab'[half]}")
                if half == 0:
                    pe.wait_ge(y_split, 2 * h + g + 1)
                    pe.wait_ge(wp_split, h + 1)
                for r in (2 * half, 2 * half + 1):
                    at = (slice(None), g, slice(r * P, (r + 1) * P))
                    last = product(job_ps(h + 1, f"proj{g}{'ab'[half]}")[:, (r % 2) * C:(r % 2 + 1) * C], yT_hi[at], yT_lo[at],
                                   wp_hi[:, par], wp_lo[:, par])
                last.then_inc(proj_ready, 1)

            pe.wait_ge(const_ready, 2)

            def transpose_x(n):
                half, kt = n // KT, n % KT
                pe.wait_ge(xn_ready, 4 * half + 4)
                for t in range(4):
                    last = pe.transpose(xT_bank(n)[:, t * P:(t + 1) * P],
                                        bias_xn(4 * half + t)[:, kt * P:(kt + 1) * P], ident[:, :])
                last.then_inc(xT_ready, 1)

            for n in range(2 * KT):
                transpose_x(n)
            for k in range(NT):
                if k % 4 == 0:
                    pe.wait_ge(xT_read, KT * (k // 4 + 1))
                project(0, 0, k)
                if k == NT - 1:
                    transpose_qk(0, 0, 0, -1)
                    transpose_qk(0, 0, 1, -1)
            project(1, 1, 0)
            transpose_qk(0, 0, 2, -1)
            project(1, 1, 1)
            transpose_qk(0, 0, 3, -1)
            score(0, 0, 0)
            pe.wait_ge(wb_ready, 1)
            for o in range(KT):
                for i in range(KT):
                    last = pe.transpose(w8T_ps[:, (i * KT + o) * P:(i * KT + o + 1) * P],
                                        wb[:, o, i * P:(i + 1) * P], ident_b[:, :])
            last.then_inc(w8T_ready, 1)

            def ffn(h, t):
                pe.wait_ge(xq_ready, t + 1)
                if isinstance(h, int) and h == 1:
                    pe.wait_ge(w8T_read, 1)
                pe.wait_ge(y_split, 2 * h)
                for kt in range(KT):
                    last = pe.matmul(yT_ps[:, 0:C], xqT[:, kt, :], w8T[:, kt, :], start=kt == 0, stop=kt == KT - 1)
                last.then_inc(ffn_ready, 1)

            def head(h, par, tile):
                first, last = isinstance(h, int) and h == 0, is_last(h)
                for s in range(NT):
                    if s < NT - 1:
                        score(h, par, s + 1)
                    elif not last:
                        score(h + 1, 1 - par, 0)
                    if s == 0:
                        if not last and not first:
                            project(h + 1, 1 - par, 0)
                        if not first:
                            attend(h - 1, 1 - par, 1, 0)
                            sum_squares(h - 1, 0, h)
                    if s == 1:
                        if not last and not first:
                            project(h + 1, 1 - par, 1)
                        if not first:
                            attend(h - 1, 1 - par, 1, 1)
                    if s == 3 and tile is not None:
                        ffn(h, tile)
                    if s in (2, 3, 4):
                        if not last:
                            project(h + 1, 1 - par, 2 * s - 2)
                        if s == 4 and not first:
                            sum_squares(h - 1, 1, h)
                        elif not first:
                            if s == 3 and tile is not None:
                                pe.wait_ge(ffn_added, tile + 1)
                            project_out(h - 1, 1 - par, 0, s - 2, h)
                        if not last:
                            project(h + 1, 1 - par, 2 * s - 1)
                    if s in (3, 4) and not last:
                        transpose_qk(h + 1, 1 - par, s - 3, h)
                    if s == 5:
                        attend(h, par, 0, 0)
                        if not last:
                            transpose_qk(h + 1, 1 - par, 2, h)
                    if s == 6:
                        if not last:
                            transpose_qk(h + 1, 1 - par, 3, h)
                        attend(h, par, 0, 1)
                        if not first:
                            project_out(h - 1, 1 - par, 1, 0, h)
                    transpose_probs(h, s)
                    if s == 7 and not first:
                        project_out(h - 1, 1 - par, 1, 1, h)

            over_heads(pe, head)
            sum_squares(H - 1, 0, H)
            project_out(H - 1, 1, 0, 0, H)
            attend(H - 1, 1, 1, 0)
            attend(H - 1, 1, 1, 1)
            project_out(H - 1, 1, 0, 1, H)
            sum_squares(H - 1, 1, H)
            project_out(H - 1, 1, 1, 0, H)
            project_out(H - 1, 1, 1, 1, H)

        @block.scalar
        def _(act):
            def copy_qkv(h, k):
                n, pair = NT * h + k, NPAIR * h + k // 2
                act.wait_ge(qkv_ready, n + 1)
                if k % 2 == 0 and not (isinstance(h, int) and h == 0):
                    last = k // 2 + 1 if isinstance(h, int) and h == 1 and k <= 2 else pair - 1
                    act.wait_ge(v_split, last)
                    act.wait_ge(qk_normed, last)
                act.activation(stage_of(h, k // 2)[:, k % 2, :], qkv_bank(h, k)[:, 0:3 * D], ACT.Copy).then_inc(qkv_read, 1)

            def square_qk(h, k):
                n = NPAIR * h + k
                act.wait_ge(qkv_read, 2 * n + 2)
                past(act, qk_meansq, n - (1 if isinstance(h, int) and h == 0 else 0))
                act.activation(squares_of(h, k), stage_of(h, k)[:, :, 0:2 * D], ACT.Square).then_inc(qk_squared, 1)

            def qk_hi(h, par, k):
                ps = first_ps(k) if isinstance(h, int) and h == 0 else job_ps(0, f"qkT{k}")
                act.wait_ge(qkT_ready, NPAIR * h + k + 1)
                at = slice(2 * k * P, (2 * k + 2) * P)
                act.activation(qT_hi[:, par, at], ps[:, 0:2 * P], ACT.Copy, scale=q_col[:, 2:3])
                act.activation(kT_hi[:, par, at], ps[:, 2 * P:4 * P], ACT.Copy).then_inc(qkT_hi_done, 1)

            def exps(h, par, s):
                i, n = ORDER[s], NT * h + s
                g, r = RANK[i]
                act.wait_ge(scores_masked, n + 1)
                act.activation(probs[:, s % 2, 0:(i + 1) * P], probs[:, s % 2, 0:(i + 1) * P], ACT.Exp,
                               bias=neg_max[:, par, s:s + 1], scale=-1.0,
                               accum_out=row_sum[:, par, g, r:r + 1]).then_inc(probs_ready, 1)

            def probs_hi(h, s):
                g, r = RANK[ORDER[s]]
                for k, (a, b) in enumerate(CHUNKS[s]):
                    act.wait_ge(pT_ready, CPH * h + CHUNK0[s] + k + 1)
                    act.activation(pT_hi[g][:, a:b, r * P:(r + 1) * P],
                                   pT_ps[(CHUNK0[s] + k) % 2][:, 0:(b - a) * P].rearrange("p (j t) -> p j t", t=P),
                                   ACT.Copy).then_inc(pT_hi_done, 1)

            def y_out(h, g):
                act.wait_ge(yT_ready, 2 * h + g + 1)
                act.activation(yT_hi[:, g, :], yT_ps[:, :], ACT.Copy).then_inc(y_hi_done, 1)
                act.activation(y_sq[:, g, :], yT_ps[:, :], ACT.Square).then_inc(y_squared, 1)

            def make_bias(h, par):
                past(act, scores_masked, NT * (h - 1))
                if isinstance(h, int) and h == 1:
                    act.wait_ge(v_split, NPAIR)
                act.activation(bias[:, par, :], dist[:, :], ACT.Copy, scale=slopes[:, bass.ds(h, 1)]
                               ).then_inc(bias_ready, 1)

            act.dma_start(q_col[:, 0:1], q_w).then_inc(small_loaded, 16)
            act.dma_start(q_col[:, 1:2], k_w).then_inc(small_loaded, 16)
            act.dma_start(q_col[:, 3:4], sub_w).then_inc(small_loaded, 16)
            act.dma_start(xs_b[:, :], ffn_xs.broadcast_to([P, 1])).then_inc(small_loaded, 16)
            act.dma_start(ffn_s[:, 2:3], ffn_ws.broadcast_to([P, 1])).then_inc(small_loaded, 16)
            act.dma_start(w8[:, :, :], ffn_w.rearrange("(k p) i -> p k i", p=P)).then_inc(w8_loaded, 16)
            act.wait_ge(w_loaded[0], 48)
            act.activation(w_hi[:, 0], w_raw[:, 0], ACT.Copy).then_inc(w_hi_done, 1)
            for n in range(2 * KT):
                half, kt = n // KT, n % KT
                act.wait_ge(xT_ready, n + 1)
                act.activation(xT_hi[:, kt, half * 512:(half + 1) * 512], xT_bank(n),
                               ACT.Copy).then_inc(xT_hi_done, 1)
            for k in range(NT):
                copy_qkv(0, k)
                if k % 2:
                    square_qk(0, k // 2)
            act.wait_ge(const_ready, 3)
            act.wait_ge(wq_col_ready, 1)
            for k in range(NPAIR):
                qk_hi(0, 0, k)
                if k == 1:
                    copy_qkv(1, 0)
                    make_bias(0, 0)
                if k == 2:
                    copy_qkv(1, 1)
            square_qk(1, 0)
            act.wait_ge(w8T_ready, 1)
            act.activation(w8T[:, :, :].rearrange("p k o -> p (k o)"), w8T_ps[:, 0:KT * C],
                           ACT.Copy).then_inc(w8T_read, 1)

            def head(h, par, tile):
                first, last = isinstance(h, int) and h == 0, is_last(h)
                for s in range(NT):
                    if s % 2:
                        exps(h, par, s)
                    if s > 0:
                        probs_hi(h, s - 1)
                    elif not first:
                        probs_hi(h - 1, NT - 1)
                    if s == 4 and not last:
                        qk_hi(h + 1, 1 - par, 0)
                    if s in (1, 2, 3, 4) and not last and not (first and s == 1):
                        copy_qkv(h + 1, [0, 1, 2, 4, 6][s])
                    if s == 6 and not last:
                        qk_hi(h + 1, 1 - par, 2)
                    if s == 0 and not last and not first:
                        copy_qkv(h + 1, 0)
                    if s % 2 == 0:
                        exps(h, par, s)
                    if s == 5 and not last:
                        qk_hi(h + 1, 1 - par, 1)
                    if s == 1 and not last and not first:
                        square_qk(h + 1, 0)
                    if s == 5 and not last:
                        make_bias(h + 1, 1 - par)
                    if s == 2 and not first:
                        if tile is not None:
                            act.wait_ge(xq_ready, tile + 1)
                        y_out(h - 1, 1)
                    if s in (2, 3, 4) and not last:
                        copy_qkv(h + 1, 2 * s - 1)
                        square_qk(h + 1, s - 1)
                    if s == 6 and not last:
                        qk_hi(h + 1, 1 - par, 3)
                    if s == 7:
                        y_out(h, 0)

            over_heads(act, head)
            probs_hi(H - 1, NT - 1)
            y_out(H - 1, 1)

        @block.vector
        def _(dve):
            steps = [0]

            def link(ins):
                steps[0] += 1
                ins.then_inc(dve_step, 1)
                dve.wait_ge(dve_step, steps[0])

            def mean_squares(h, k):
                n = NPAIR * h + k
                dve.wait_ge(qk_squared, n + 1)
                past(dve, qk_normed, n - 1)
                dve.tensor_reduce(qk_ms[:, k % 2, :], squares_of(h, k).rearrange("p t (a d) -> p (t a) d", d=D),
                                  AX.X, ALU.add).then_inc(qk_summed, 1)
                dve.wait_ge(qk_summed, n + 1)
                dve.tensor_scalar(qk_ms[:, k % 2, :], qk_ms[:, k % 2, :], 1.0 / D, EPS,
                                  ALU.mult, ALU.add).then_inc(qk_meansq, 1)

            def split_v(h, par, k):
                n = NPAIR * h + k
                dve.wait_ge(qkv_read, 2 * n + 2)
                past(dve, yT_ready, 2 * (h - 1))
                v = stage_of(h, k)[:, :, 2 * D:3 * D]
                dve.tensor_copy(v_hi[:, par, 2 * k:2 * k + 2, :], v).then_inc(v_hi_done, 1)
                dve.wait_ge(v_hi_done, n + 1)
                dve.tensor_tensor(v_lo[:, par, 2 * k:2 * k + 2, :], v, v_hi[:, par, 2 * k:2 * k + 2, :].bitcast(f32),
                                  ALU.subtract).then_inc(v_split, 1)

            def qk_lo(h, par, k):
                ps = first_ps(k) if isinstance(h, int) and h == 0 else job_ps(0, f"qkT{k}")
                dve.wait_ge(qkT_hi_done, NPAIR * h + k + 1)
                at = slice(2 * k * P, (2 * k + 2) * P)
                dve.scalar_tensor_tensor(qT_lo[:, par, at], ps[:, 0:2 * P], q_col[:, 2:3],
                                         qT_hi[:, par, at].bitcast(f32), ALU.mult, ALU.subtract)
                dve.tensor_tensor(kT_lo[:, par, at], ps[:, 2 * P:4 * P], kT_hi[:, par, at].bitcast(f32),
                                  ALU.subtract).then_inc(misc_read, 1)

            def mask(h, par, s):
                i, n = ORDER[s], NT * h + s
                ps, at, _ = score_at(i)
                w = (i + 1) * P
                dve.wait_ge(scores_ready, n + 1)
                if s == 0:
                    dve.wait_ge(bias_ready, h + 1)
                s2, h2 = (s - 2, h) if s >= 2 else (s - 2 + NT, h - 1)
                past(dve, pT_ready, CPH * h2 + CHUNK0[s2 + 1])
                dve.nop(nofuse=True)
                dve.tensor_tensor_reduce(out=probs[:, s % 2, 0:w], in0=ps[:, at:at + w],
                                         in1=bias[:, par, (NT - 1 - i) * P:(NT - 1 - i) * P + w],
                                         scale=1.0, scalar=3.0e38, op0=ALU.add, op1=ALU.min,
                                         accum_out=neg_max[:, par, s:s + 1]).then_inc(scores_masked, 1)

            def probs_lo(h, s):
                g, r = RANK[ORDER[s]]
                for k, (a, b) in enumerate(CHUNKS[s]):
                    dve.wait_ge(pT_hi_done, CPH * h + CHUNK0[s] + k + 1)
                    dve.tensor_tensor(pT_lo[g][:, a:b, r * P:(r + 1) * P],
                                      pT_ps[(CHUNK0[s] + k) % 2][:, 0:(b - a) * P].rearrange("p (j t) -> p j t", t=P),
                                      pT_hi[g][:, a:b, r * P:(r + 1) * P].bitcast(f32),
                                      ALU.subtract).then_inc(pT_split, 1)

            def y_lo(h, g):
                dve.wait_ge(y_squared, 2 * h + g + 1)
                dve.tensor_tensor(yT_lo[:, g, :], yT_ps[:, :], yT_hi[:, g, :].bitcast(f32),
                                  ALU.subtract).then_inc(y_split, 1)

            def y_mean(h, par, g):
                dve.scalar_tensor_tensor(y_el2[:, g, :], row_sum[:, par, g, :], EPS, row_sum[:, par, g, :],
                                         ALU.mult, ALU.mult).then_inc(el2_ready, 1)
                dve.wait_ge(el2_ready, 2 * h + g + 1)
                dve.wait_ge(ss_ready, 2 * h + g + 1)
                dve.scalar_tensor_tensor(y_ms[:, g, :], job_ps(h + 1, f"ss{g}")[:, 0:4], 1.0 / D, y_el2[:, g, :],
                                         ALU.mult, ALU.add).then_inc(misc_read, 1)

            def add_out(h, g, half):
                dve.wait_ge(proj_ready, 4 * h + 2 * g + half + 1)
                dve.wait_ge(y_normed, 2 * h + g + 1)
                for r in (2 * half, 2 * half + 1):
                    t = GROUPS[g][r]
                    last = dve.scalar_tensor_tensor(acc[:, t, :], job_ps(h + 1, f"proj{g}{'ab'[half]}")[:, (r % 2) * C:(r % 2 + 1) * C],
                                                    y_r[:, g, r:r + 1], acc[:, t, :], ALU.mult, ALU.add)
                last.then_inc(misc_read, 1)

            for n in range(2):
                tiles = range(n * NT // 2, (n + 1) * NT // 2)
                at = slice(tiles[0], tiles[-1] + 1)
                dve.wait_ge(x_loaded[n], 16)
                for t in tiles:
                    last = dve.bn_stats(stats[:, t, :], acc[:, t, :])
                link(last)
                for t in tiles:
                    last = dve.bn_aggr(mean_var[:, t, :], stats[:, t, :])
                link(last)
                dve.tensor_scalar(rstd[:, at], mean_var[:, at, 1], EPS, None, ALU.add).then_inc(var_ready, 1)

            for n in range(2):
                dve.wait_ge(rstd_ready, n + 1)
                for t in range(n * NT // 2, (n + 1) * NT // 2):
                    dve.tensor_scalar(bias_xn(t), acc[:, t, :], mean_var[:, t, 0:1], rstd[:, t:t + 1],
                                      ALU.subtract, ALU.mult).then_inc(xn_ready, 1)
            dve.wait_ge(small_loaded, 80)
            dve.scalar_tensor_tensor(q_col[:, 2:3], q_col[:, 0:1], -SCALE, q_col[:, 1:2],
                                     ALU.mult, ALU.mult).then_inc(wq_col_ready, 1)
            for n in range(2 * KT):
                half, kt = n // KT, n % KT
                at = slice(half * 512, (half + 1) * 512)
                if n == 1:
                    dve.wait_ge(w_hi_done, 1)
                    dve.tensor_tensor(w_lo[:, 0], w_raw[:, 0], w_hi[:, 0].bitcast(f32),
                                      ALU.subtract).then_inc(w_split, 1)
                dve.wait_ge(xT_hi_done, n + 1)
                dve.tensor_tensor(xT_lo[:, kt, at], xT_bank(n), xT_hi[:, kt, at].bitcast(f32),
                                  ALU.subtract).then_inc(xT_read, 1)

            def quantize_x(t):
                u, m = (y_sq[:, 1, i * 2 * P:(i + 1) * 2 * P] for i in range(2))
                tokens = slice(t * P, (t + 1) * P) if isinstance(t, int) else bass.ds(t * P, P)
                parts = (xT_hi[:, :, tokens], xT_lo[:, :, tokens])

                def then(step, ins):
                    ins.then_inc(x_stepped, 1)
                    dve.wait_ge(x_stepped, t * 6 + step)

                flat = "p (k t) -> p k t"
                then(1, dve.tensor_tensor(u.rearrange(flat, t=P), parts[0].bitcast(f32), parts[1].bitcast(f32), ALU.add))
                then(2, dve.tensor_scalar(u, u, ffn_s[:, 1:2], E4M3_MAX, ALU.mult, ALU.min))
                then(3, dve.tensor_scalar(u, u, -E4M3_MAX, None, ALU.max))
                then(4, dve.tensor_scalar(m.bitcast(i32), u.bitcast(i32), 0x7F800000, None, ALU.bitwise_and))
                then(5, dve.tensor_scalar(m, m, 2.0 ** -6, 1.5 * 2.0 ** 20, ALU.max, ALU.mult))
                then(6, dve.tensor_tensor(u, u, m, ALU.add))
                dve.tensor_tensor(xqT[:, :, :].rearrange("p k t -> p (k t)"), u, m, ALU.subtract).then_inc(xq_ready, 1)

            u = probs[:, :, :].rearrange("p a t -> p (a t)")
            dve.wait_ge(w8_loaded, 16)
            code = u[:, 0:KT * C].bitcast(i32)
            mag = u[:, KT * C:2 * KT * C]
            alt = u[:, 2 * KT * C:3 * KT * C]
            sign = u[:, 3 * KT * C:4 * KT * C]
            link(dve.tensor_copy(code, w8[:, :, :].rearrange("p k i -> p (k i)")))
            dve.tensor_scalar(sign, code, 128, -2.0, ALU.is_ge, ALU.mult)
            link(dve.tensor_scalar(mag.bitcast(i32), code, 0x7F, 20, ALU.bitwise_and, ALU.logical_shift_left))
            link(dve.tensor_scalar(mag.bitcast(i32), mag.bitcast(i32), 112 << 23, None, ALU.bitwise_or))
            link(dve.tensor_scalar(mag, mag, 256.0, None, ALU.mult))
            link(dve.tensor_scalar(alt, mag, 2.0, -(2.0 ** -6), ALU.mult, ALU.add))
            link(dve.tensor_tensor(mag, mag, alt, ALU.min))
            dve.scalar_tensor_tensor(wb[:, :, :].rearrange("p k i -> p (k i)"), sign, 1.0, mag,
                                     ALU.add, ALU.mult).then_inc(wb_ready, 1)
            link(dve.tensor_copy(ffn_s[:, 0:1], xs_b[:, :]))
            link(dve.reciprocal(ffn_s[:, 1:2], ffn_s[:, 0:1]))
            dve.tensor_tensor(ffn_s[:, 3:4], ffn_s[:, 0:1], ffn_s[:, 2:3], ALU.mult)
            def norm_first(k):
                dve.wait_ge(qk_r_ready, k + 1)
                past(dve, qkT_ready, k - 1)
                scale_qk(dve, 0, k)

            mean_squares(0, 0)
            split_v(0, 0, 0)
            mean_squares(0, 1)
            norm_first(0)
            mean_squares(0, 2)
            norm_first(1)
            mean_squares(0, 3)
            qk_lo(0, 0, 0)
            norm_first(2)
            norm_first(3)
            qk_lo(0, 0, 1)
            qk_lo(0, 0, 2)
            qk_lo(0, 0, 3)
            mask(0, 0, 0)
            for k in (1, 2, 3):
                split_v(0, 0, k)

            def add_ffn(t):
                dve.wait_ge(ffn_ready, t + 1)
                rows = acc[:, t, :] if isinstance(t, int) else acc[:, bass.ds(t, 1), :].rearrange("p t c -> p (t c)")
                dve.scalar_tensor_tensor(rows, yT_ps[:, 0:C], ffn_s[:, 3:4], rows, ALU.mult, ALU.add
                                         ).then_inc(ffn_added, 1)

            def head(h, par, tile):
                first, last = isinstance(h, int) and h == 0, is_last(h)
                for s in range(NT):
                    if s == 3 and tile is not None:
                        add_ffn(tile)
                    if s in (3, 5) and not last:
                        mean_squares(h + 1, 1 if s == 3 else 3)
                    if s > 0:
                        probs_lo(h, s - 1)
                    if s in (4, 5) and not last:
                        qk_lo(h + 1, 1 - par, s - 4)
                    if s == 6 and not last:
                        qk_lo(h + 1, 1 - par, 2)
                    if s == NT - 1:
                        y_lo(h, 0)
                        probs_lo(h, NT - 1)
                    if s < NT - 1:
                        mask(h, par, s + 1)
                    elif not last:
                        mask(h + 1, 1 - par, 0)
                    if s == 0 and not first:
                        if not (isinstance(h, int) and h == 1):
                            add_out(h - 2, 1, 1)
                        y_mean(h - 1, 1 - par, 0)
                    if s == 0 and tile is not None:
                        quantize_x(tile)
                    if s == 6 and not last:
                        qk_lo(h + 1, 1 - par, 3)
                    if s == 1 and not last:
                        mean_squares(h + 1, 0)
                    if s == 4 and not first:
                        y_mean(h - 1, 1 - par, 1)
                    if s in (2, 3, 4, 5) and not last:
                        split_v(h + 1, 1 - par, s - 2)
                    if s in (2, 3) and not first:
                        add_out(h - 1, 0, s - 2)
                    if s == 3 and not last:
                        mean_squares(h + 1, 2)
                    if s == 2 and not first:
                        y_lo(h - 1, 1)
                    if s == 6 and not first:
                        add_out(h - 1, 1, 0)

            over_heads(dve, head)
            add_out(H - 2, 1, 1)
            y_mean(H - 1, 1, 0)
            add_out(H - 1, 0, 0)
            y_lo(H - 1, 1)
            add_out(H - 1, 0, 1)
            y_mean(H - 1, 1, 1)
            add_out(H - 1, 1, 0)
            add_out(H - 1, 1, 1)


def kernel(L0_attn_x, L0_attn_Wq, L0_attn_Wk, L0_attn_Wv, L0_attn_Wproj, L0_attn_q_rms_w, L0_attn_k_rms_w,
           L0_attn_subln_w, L0_ffn_weight, L0_ffn_weight_scale, L0_ffn_input_scale):
    import concourse.bacc as bacc
    from concourse.bass_utils import run_bass_kernel_spmd

    nc = bacc.Bacc("TRN2", target_bir_lowering=False, num_devices=1)
    shaped = {
        "x": np.asarray(L0_attn_x)[0],
        "wq": L0_attn_Wq, "wk": L0_attn_Wk, "wv": L0_attn_Wv, "wproj": L0_attn_Wproj,
        "q_w": np.asarray(L0_attn_q_rms_w).reshape(-1, 1),
        "k_w": np.asarray(L0_attn_k_rms_w).reshape(-1, 1),
        "sub_w": np.asarray(L0_attn_subln_w).reshape(-1, 1),
        "ffn_w": np.asarray(L0_ffn_weight).view(np.uint8),
        "ffn_ws": np.asarray(L0_ffn_weight_scale).reshape(1, 1),
        "ffn_xs": np.asarray(L0_ffn_input_scale).reshape(1, 1),
    }
    arrays, aps = {}, {}
    for name, a in shaped.items():
        a = np.ascontiguousarray(a)
        arrays["in_" + name] = a
        aps[name] = nc.dram_tensor("in_" + name, a.shape, mybir.dt.from_np(a.dtype), kind="ExternalInput").ap()
    rows, cols = shaped["x"].shape
    out = nc.dram_tensor("out", (rows, cols), mybir.dt.float32, kind="ExternalOutput").ap()
    build_block(nc, out=out, **aps)
    got = run_bass_kernel_spmd(nc, [arrays], core_ids=[0])
    return got.results[0]["out"].reshape(1, rows, cols)
```
